# Optimizing a Trainium2 kernel written in Bass

```python
import numpy as np
import jax
import jax.numpy as jnp

def _softmax(x, axis=-1):
    return jax.nn.softmax(x, axis=axis)

def _gelu(x):
    return jax.nn.gelu(x, approximate=True)

def _silu(x):
    return jax.nn.silu(x)

def _sigmoid(x):
    return jax.nn.sigmoid(x)

def _layernorm(x, axis=-1, eps=1e-05):
    m = jnp.mean(x, axis=axis, keepdims=True)
    v = jnp.var(x, axis=axis, keepdims=True)
    return (x - m) / jnp.sqrt(v + eps)

def _scatter_add(tgt, idx, src, axis=0):
    return tgt.at[idx].add(src)

def _segment_sum(src, seg, n):
    return jax.ops.segment_sum(src, seg, n)
kernel_name = 'mk_xattn_ffn_d1_seqx_r2_2a8f8b'

def setup_inputs(seed: int=0):
    np.random.seed(seed)
    _w = jnp.asarray

    def _rec_inputs():
        import jax
        import jax.numpy as jnp
        _rk = jax.random.key(seed)
        x = 7.22e-05 + 1 * jax.random.normal(jax.random.fold_in(_rk, 1), (32, 256, 512), jnp.float32)
        _lenS = 256 - jax.random.randint(jax.random.fold_in(_rk, 7), (32,), 0, max(1, 256 // 4) + 1, jnp.int32)
        _lenS2 = 256 - jax.random.randint(jax.random.fold_in(_rk, 8), (32,), 0, max(1, 256 // 4) + 1, jnp.int32)
        _ctx_1024P = jax.random.normal(jax.random.fold_in(_rk, 11), (32, 16, 512), jnp.float32)
        _ctx_1024c = jax.random.dirichlet(jax.random.fold_in(_rk, 511), 0.3 * jnp.ones((16,), jnp.float32), (32, 256))
        _ctx_1024t = jnp.einsum('bsk,bkd->bsd', _ctx_1024c, _ctx_1024P)
        _ctx_1024t = _ctx_1024t * jax.lax.rsqrt(jnp.mean(jnp.square(_ctx_1024t)) + 1e-12) * 0.953939
        ctx_1024 = 4.13588e-05 + 0.999923 * (_ctx_1024t + 0.3 * jax.random.normal(jax.random.fold_in(_rk, 611), (32, 256, 512), jnp.float32))
        _validS = jnp.arange(256)[None, :] < _lenS[:, None]
        _validS2 = jnp.arange(256)[None, :] < _lenS2[:, None]
        _causal = jnp.tril(jnp.ones((256, 256), dtype=bool))
        mask_SxS2_bk0 = jnp.logical_not(jnp.broadcast_to(_validS2[0:1, :], (256, 256)))
        return (x, ctx_1024, mask_SxS2_bk0)
    x, ctx_1024, mask_SxS2_bk0 = _rec_inputs()

    def _L0_xattn_setup():
        import jax, jax.numpy as jnp
        import numpy as np
        D_MODEL = 512
        NUM_HEADS = 16
        D_K = D_MODEL // NUM_HEADS
        B, S = (4, 1024)
        key = jax.random.key(seed)
        ks = jax.random.split(key, 12)
        std = 1.0 / np.sqrt(D_MODEL)
        inp = {'q': jax.random.normal(ks[0], (B, S, D_MODEL), dtype=jnp.float32), 'k': jax.random.normal(ks[1], (B, S, D_MODEL), dtype=jnp.float32), 'v': jax.random.normal(ks[2], (B, S, D_MODEL), dtype=jnp.float32), 'mask': jnp.tril(jnp.ones((S, S), dtype=bool)), 'wq': jax.random.normal(ks[3], (D_MODEL, D_MODEL), dtype=jnp.float32) * std, 'bq': jnp.zeros((D_MODEL,), dtype=jnp.float32), 'wk': jax.random.normal(ks[4], (D_MODEL, D_MODEL), dtype=jnp.float32) * std, 'bk': jnp.zeros((D_MODEL,), dtype=jnp.float32), 'wv': jax.random.normal(ks[5], (D_MODEL, D_MODEL), dtype=jnp.float32) * std, 'bv': jnp.zeros((D_MODEL,), dtype=jnp.float32), 'wo': jax.random.normal(ks[6], (D_MODEL, D_MODEL), dtype=jnp.float32) * std, 'bo': jnp.zeros((D_MODEL,), dtype=jnp.float32)}
        return inp
    _L0_xattn_all = _L0_xattn_setup()
    _L0_xattn_in = {k: v for k, v in _L0_xattn_all.items() if k in ('wq', 'bq', 'wk', 'bk', 'wv', 'bv', 'wo', 'bo')}
    del _L0_xattn_all

    def _L0_ffn_setup():
        import jax, jax.numpy as jnp
        import numpy as np
        N_EMBD = 512
        N_EXP = 8
        TOP_K = 2
        CAPACITY = 2048
        D_FF = 3 * N_EMBD
        key = jax.random.key(seed)
        k1, k2, k3, k4 = jax.random.split(key, 4)
        x = jax.random.normal(k1, (8, 1024, N_EMBD), dtype=jnp.float32)
        w_gate = jax.random.normal(k2, (N_EMBD, N_EXP), dtype=jnp.float32) * 0.02
        c_fc = jax.random.normal(k3, (N_EXP, N_EMBD, D_FF), dtype=jnp.float32) * 0.02
        c_proj = jax.random.normal(k4, (N_EXP, D_FF // 2, N_EMBD), dtype=jnp.float32) * 0.02
        return {'x': x, 'w_gate': w_gate, 'c_fc': c_fc, 'c_proj': c_proj}
    _L0_ffn_all = _L0_ffn_setup()
    _L0_ffn_in = {k: v for k, v in _L0_ffn_all.items() if k in ('w_gate', 'c_fc', 'c_proj')}
    del _L0_ffn_all
    return {'x': x, 'ctx_1024': ctx_1024, 'mask_SxS2_bk0': mask_SxS2_bk0, 'L0_xattn_wq': _L0_xattn_in['wq'], 'L0_xattn_bq': _L0_xattn_in['bq'], 'L0_xattn_wk': _L0_xattn_in['wk'], 'L0_xattn_bk': _L0_xattn_in['bk'], 'L0_xattn_wv': _L0_xattn_in['wv'], 'L0_xattn_bv': _L0_xattn_in['bv'], 'L0_xattn_wo': _L0_xattn_in['wo'], 'L0_xattn_bo': _L0_xattn_in['bo'], 'L0_ffn_w_gate': _L0_ffn_in['w_gate'], 'L0_ffn_c_fc': _L0_ffn_in['c_fc'], 'L0_ffn_c_proj': _L0_ffn_in['c_proj']}

def reference(x, ctx_1024, mask_SxS2_bk0, L0_xattn_wq, L0_xattn_bq, L0_xattn_wk, L0_xattn_bk, L0_xattn_wv, L0_xattn_bv, L0_xattn_wo, L0_xattn_bo, L0_ffn_w_gate, L0_ffn_c_fc, L0_ffn_c_proj):
    import jax
    import jax.numpy as jnp

    def _L0_xattn_ref(q, k, v, mask, wq, bq, wk, bk, wv, bv, wo, bo):
        import jax, jax.numpy as jnp
        import numpy as np
        D_MODEL = 512
        NUM_HEADS = 16
        D_K = D_MODEL // NUM_HEADS
        B, S = (4, 1024)
        b, s, d = q.shape

        def proj(x, w, bias):
            return (x @ w.T + bias).reshape(b, -1, NUM_HEADS, D_K).transpose(0, 2, 1, 3)
        qh = proj(q, wq, bq)
        kh = proj(k, wk, bk)
        vh = proj(v, wv, bv)
        scale = 1.0 / np.sqrt(D_K)
        scores = jnp.einsum('bhqd,bhkd->bhqk', qh, kh) * scale
        scores = jnp.where(mask[None, None, :, :], scores, -1000000000.0)
        probs = jax.nn.softmax(scores, axis=-1)
        out = jnp.einsum('bhqk,bhkd->bhqd', probs, vh)
        out = out.transpose(0, 2, 1, 3).reshape(b, s, d)
        return out @ wo.T + bo

    def _L0_ffn_ref(x, w_gate, c_fc, c_proj):
        import jax, jax.numpy as jnp
        import numpy as np
        N_EMBD = 512
        N_EXP = 8
        TOP_K = 2
        CAPACITY = 2048
        D_FF = 3 * N_EMBD
        B, T, d = x.shape
        N = B * T
        xf = x.reshape(N, d)
        scores = jax.nn.softmax(xf @ w_gate, axis=-1)
        weights, idx = jax.lax.top_k(scores, TOP_K)
        flat_e = idx.reshape(-1)
        tok = jnp.repeat(jnp.arange(N), TOP_K)
        oh = jax.nn.one_hot(flat_e, N_EXP, dtype=jnp.int32)
        pos = (jnp.cumsum(oh, axis=0) * oh).sum(-1) - 1
        valid = pos < CAPACITY
        pos_c = jnp.where(valid, pos, 0)
        vmask = valid.astype(x.dtype)[:, None]
        exp_x = jnp.zeros((N_EXP, CAPACITY, d), x.dtype)
        exp_x = exp_x.at[flat_e, pos_c].add(xf[tok] * vmask)
        h = jnp.einsum('ecd,edf->ecf', exp_x, c_fc)
        a, g = jnp.split(h, 2, axis=-1)
        h = jax.nn.silu(a) * g
        exp_out = jnp.einsum('ecf,efd->ecd', h, c_proj)
        gathered = exp_out[flat_e, pos_c]
        w = weights.reshape(-1)[:, None] * vmask
        out = (gathered * w).reshape(N, TOP_K, d).sum(axis=1)
        return out.reshape(B, T, d)
    x = x + _L0_xattn_ref(_layernorm(x, axis=-1), ctx_1024, ctx_1024, mask_SxS2_bk0, L0_xattn_wq, L0_xattn_bq, L0_xattn_wk, L0_xattn_bk, L0_xattn_wv, L0_xattn_bv, L0_xattn_wo, L0_xattn_bo)
    x = x + _L0_ffn_ref(_layernorm(x, axis=-1), L0_ffn_w_gate, L0_ffn_c_fc, L0_ffn_c_proj)
    return x

_drawn_inputs = setup_inputs


def setup_inputs(seed=0):
    import zlib

    import numpy as np

    out = dict(_drawn_inputs(seed))
    spreads = {'L0_xattn_bq': (0.0, 0.327),
     'L0_xattn_bk': (0.0, 0.8),
     'L0_xattn_bv': (0.0, 0.1),
     'L0_xattn_bo': (0.0, 0.1)}
    factors = {'L0_ffn_w_gate': 4.516, 'L0_ffn_c_fc': 3.981, 'L0_ffn_c_proj': 3.98}
    for name, (base, spread) in spreads.items():
        noise = np.random.default_rng([zlib.crc32(name.encode()), seed]).standard_normal(out[name].shape)
        drawn = base * np.exp(spread * noise) if base else spread * noise
        out[name] = jnp.asarray(drawn.astype(out[name].dtype))
    for name, factor in factors.items():
        out[name] = (out[name] * factor).astype(out[name].dtype)
    return out
```

```python
import concourse.bass as bass
from concourse import mybir

F32 = mybir.dt.float32
F32R = mybir.dt.float32r
I32 = mybir.dt.int32
U32 = mybir.dt.uint32
U8 = mybir.dt.uint8
ALU = mybir.AluOpType
ACT = mybir.ActivationFunctionType
X_AXIS = mybir.AxisListType.X

P = 128
BATCH, SEQ, D = 32, 256, 512
HEADS, DK = 16, 32
TILES = SEQ // P
DC = D // P
HPC = P // DK
TOKENS = BATCH * SEQ
EXPERTS, TOP_K, CAPACITY = 8, 2, 2048
DFF = 3 * D
GATE = DFF // 2
MC = GATE // P
SLOTS = CAPACITY // P
CHUNK = 512
CT = CHUNK // P
CHUNKS = CAPACITY // CHUNK
LN_EPS = 1e-5
MASKED = 1e9
OVER = float(1 << 20)
SCALE = float(DK) ** -0.5
LAG = 3
PASSES = ((0, 0), (0, 1), (1, 0))


def need(eng, sem, value):
    if isinstance(value, int) and value <= 0:
        return
    eng.wait_ge(sem, value)


def is_step(n, number):
    return isinstance(n, int) and n == number


def settle(eng):
    eng.nop(nofuse=True)


def attention_block(nc, x, ctx_t, mask, w_attn, b_qk, b_v, b_o, w_gate, out, xn2_rows, table):
    from contextlib import ExitStack
    x_rows = x.rearrange("(b t p) d -> b p t d", t=TILES, p=P)
    out_rows = out[0:TOKENS, :].rearrange("(b t p) d -> b p t d", t=TILES, p=P)
    xn2_out = xn2_rows[0:TOKENS, :].rearrange("(b t p) d -> b p t d", t=TILES, p=P)
    with ExitStack() as stack:
        def sb(name, shape, dt=F32):
            return stack.enter_context(nc.sbuf_tensor(name, shape, dt))

        def ps(name, shape):
            return stack.enter_context(nc.psum_tensor(name, shape, F32))

        def sem(name):
            return stack.enter_context(nc.semaphore(name))

        w_hi = sb("w_hi", [P, 4, DC, D], F32R)
        w_lo = sb("w_lo", [P, 4, DC, D], F32R)
        w_raw = sb("w_raw", [P, DC, D])
        w_parts = (w_hi, w_lo)
        wg = sb("wg", [P, DC, EXPERTS])
        bias_qk = sb("bias_qk", [P, 2, DC])
        bias_v = sb("bias_v", [P, D])
        bias_o = sb("bias_o", [P, D])
        mask_u8 = sb("mask_u8", [P, TILES, SEQ], U8)
        mask_add = sb("mask_add", [P, TILES, SEQ])
        row_any = sb("row_any", [P, TILES])
        ident = sb("ident", [P, P])
        before = sb("before", [P, P])
        ones = sb("ones", [P, P])
        expert_ids = sb("expert_ids", [P, EXPERTS])
        list_base = sb("list_base", [P, TILES, EXPERTS])
        half_pow = sb("half_pow", [P, TILES])
        tok_ids = sb("tok_ids", [P, TILES])
        zeros = sb("zeros", [P, D])
        default_rec = sb("default_rec", [P, SLOTS, 2], I32)

        xin = sb("xin", [P, 2, TILES, D])
        xn = sb("xn", [P, TILES, D])
        xt = [sb("xt_hi", [P, DC, SEQ], F32R), sb("xt_lo", [P, DC, SEQ], F32R)]
        x_bo = sb("x_bo", [P, TILES, D])
        cin = sb("cin", [P, 2, DC, SEQ])
        ct = [sb("ct_hi", [P, 2, DC, SEQ], F32R), sb("ct_lo", [P, 2, DC, SEQ], F32R)]
        qt = sb("qt", [P, 2, DC, SEQ])
        kt = sb("kt", [P, 2, DC, SEQ])
        v = sb("v", [P, 2, TILES, D])
        neg_scores = sb("neg_scores", [P, 2, TILES, SEQ])
        probs = sb("probs", [P, 4, TILES, SEQ])
        probs_t = sb("probs_t", [P, 2, TILES, SEQ])
        low = sb("low", [P, 4, TILES])
        row_sum = sb("row_sum", [P, 4, TILES])
        row_inv = sb("row_inv", [P, 4, TILES])
        at = [sb("at_hi", [P, DC, SEQ], F32R), sb("at_lo", [P, DC, SEQ], F32R)]
        x2 = sb("x2", [P, TILES, D])
        xn2 = sb("xn2", [P, TILES, D])
        x2t = sb("x2t", [P, DC, SEQ])
        stats = sb("stats", [P, 2, TILES, 6])
        moments = sb("moments", [P, 2, TILES, 2])
        shifted = sb("shifted", [P, 2, TILES])
        rstd = sb("rstd", [P, 2, TILES])
        logits = sb("logits", [P, TILES, EXPERTS])
        top = sb("top", [P, TILES, 8])
        top_at = sb("top_at", [P, TILES, 8], U32)
        top_id = sb("top_id", [P, TILES, TOP_K])
        chosen = sb("chosen", [P, TILES, TOP_K, EXPERTS])
        member = sb("member", [P, TILES, EXPERTS])
        members_before = sb("members_before", [P, EXPERTS])
        fall = sb("fall", [P, TILES, 8])
        weight_exp = sb("weight_exp", [P, TILES, 8])
        weight_sum = sb("weight_sum", [P, TILES])
        weight_inv = sb("weight_inv", [P, TILES])
        over = sb("over", [P, TILES, EXPERTS])
        place = sb("place", [P, TILES, EXPERTS])
        place_k = sb("place_k", [P, TILES, TOP_K, EXPERTS])
        place_f = sb("place_f", [P, TILES, TOP_K])
        place_i = sb("place_i", [P, TILES, TOP_K], I32)
        rec = sb("rec", [P, TILES, TOP_K, 2], I32)

        scores_ps = [ps(f"scores_ps{i}", [P, TILES, SEQ]) for i in range(2)]
        probs_t_ps = [ps(f"probs_t_ps{i}", [P, TILES, SEQ]) for i in range(2)]
        attn_ps = [ps(f"attn_ps{i}", [P, 512]) for i in range(2)]
        bank_a = ps("bank_a", [P, 512])
        bank_b = ps("bank_b", [P, 512])

        setup_loaded = sem("setup_loaded")
        w_loaded = sem("w_loaded")
        w_hi_done = sem("w_hi_done")
        w_split = sem("w_split")
        pool_const = sem("pool_const")
        dve_const = sem("dve_const")
        defaults_stored = sem("defaults_stored")
        x_loaded = [sem(f"x_loaded{i}") for i in range(2)]
        c_loaded = [sem(f"c_loaded{i}") for i in range(2)]
        ln1_step = sem("ln1_step")
        ln1_var = sem("ln1_var")
        ln1_shift = sem("ln1_shift")
        ln1_rstd = sem("ln1_rstd")
        xn_ready = sem("xn_ready")
        xt_full = sem("xt_full")
        xt_hi_done = sem("xt_hi_done")
        xt_split = sem("xt_split")
        ct_hi_done = sem("ct_hi_done")
        ct_split = sem("ct_split")
        xbo_ready = sem("xbo_ready")
        q_full = sem("q_full")
        k_full = sem("k_full")
        v_full = sem("v_full")
        q_ready = sem("q_ready")
        k_ready = sem("k_ready")
        v_ready = sem("v_ready")
        scored = sem("scored")
        masked = sem("masked")
        exped = sem("exped")
        inverted = sem("inverted")
        normed = sem("normed")
        turned = sem("turned")
        turned_copied = sem("turned_copied")
        attended = sem("attended")
        at_hi_done = sem("at_hi_done")
        at_split = sem("at_split")
        wo_full = sem("wo_full")
        x2_ready = sem("x2_ready")
        x2_stored = sem("x2_stored")
        ln2_step = sem("ln2_step")
        ln2_var = sem("ln2_var")
        ln2_shift = sem("ln2_shift")
        ln2_rstd = sem("ln2_rstd")
        xn2_ready = sem("xn2_ready")
        xn2_stored = sem("xn2_stored")
        x2t_full = sem("x2t_full")
        x2t_ready = sem("x2t_ready")
        logits_full = sem("logits_full")
        logits_copied = sem("logits_copied")
        route_step = sem("route_step")
        member_ready = sem("member_ready")
        fall_ready = sem("fall_ready")
        weight_exped = sem("weight_exped")
        place_full = sem("place_full")
        place_used = sem("place_used")
        place_step = sem("place_step")
        rec_ready = sem("rec_ready")
        rec_stored = sem("rec_stored")

        def steps(eng, step):
            for n in range(-2, LOOPED):
                step(n, n % 2)
            with eng.Fori(LOOPED // 2, (BATCH - 3) // 2) as j:
                step(j * 2 + 1, 1, inner=True)
                step(j * 2 + 2, 0, inner=True)
            for n in range(BATCH - 3, BATCH + 1):
                step(n, n % 2)

        LOOPED = 3

        def has(n, inner, ahead):
            return inner or 0 <= n + ahead < BATCH

        with nc.Block() as block:

            @block.sync
            def _(sp):
                sp.dma_start(wg[:, :, :], w_gate).then_inc(setup_loaded, 16)
                sp.dma_start(bias_qk[:, :, :], b_qk).then_inc(setup_loaded, 16)
                sp.dma_start(bias_v[:, :], b_v).then_inc(setup_loaded, 16)
                sp.dma_start(bias_o[:, :], b_o).then_inc(setup_loaded, 16)
                sp.dma_start(mask_u8[:, :, :], mask.rearrange("(t p) k -> p t k", p=P)).then_inc(setup_loaded, 16)

                def load(n, p):
                    need(sp, ct_split, DC * (n - 1))
                    sp.dma_start(cin[:, p, :, :], ctx_t[n]).then_inc(c_loaded[p], 16)
                    need(sp, xn_ready, n - 1)
                    need(sp, xbo_ready, n - 1)
                    sp.dma_start(xin[:, p, :, :], x_rows[n]).then_inc(x_loaded[p], 16)

                def step(n, p, inner=False):
                    if has(n, inner, 2):
                        load(n + 2, p)
                    if is_step(n, -2):
                        for m in range(4):
                            need(sp, w_split, m)
                            sp.dma_start(w_raw[:, :, :], w_attn[m]).then_inc(w_loaded, 16)
                        sp.wait_ge(pool_const, 8)
                        for e in range(EXPERTS):
                            sp.dma_start(table[e * CAPACITY:(e + 1) * CAPACITY, :].rearrange(
                                "(p s) r -> p s r", p=P), default_rec[:, :, :]).then_inc(defaults_stored, 16)
                        sp.dma_start(out[TOKENS:TOKENS + P, :], zeros[:, :]).then_inc(defaults_stored, 16)
                        sp.dma_start(xn2_rows[TOKENS:TOKENS + P, :], zeros[:, :]).then_inc(defaults_stored, 16)
                    if has(n, inner, -1):
                        sp.wait_ge(x2_ready, n * TILES)
                        sp.dma_start(out_rows[n - 1], x2[:, :, :]).then_inc(x2_stored, 16)
                        sp.wait_ge(xn2_ready, n)
                        sp.dma_start(xn2_out[n - 1], xn2[:, :, :]).then_inc(xn2_stored, 16)
                steps(sp, step)
                sp.wait_ge(defaults_stored, 16 * (EXPERTS + 2))
                sp.wait_ge(x2_stored, 16 * BATCH)
                sp.wait_ge(xn2_stored, 16 * BATCH)

            @block.gpsimd
            def _(pool):
                nc.gpsimd.memset(ident[:, :], 0.0).then_inc(pool_const, 1)
                nc.gpsimd.memset(before[:, :], 0.0).then_inc(pool_const, 1)
                nc.gpsimd.memset(zeros[:, :], 0.0).then_inc(pool_const, 1)
                nc.gpsimd.iota(default_rec[:, :, 0], pattern=[[0, SLOTS]], base=TOKENS,
                               channel_multiplier=1).then_inc(pool_const, 1)
                nc.gpsimd.iota(default_rec[:, :, 1], pattern=[[0, SLOTS]], base=0,
                               channel_multiplier=0).then_inc(pool_const, 1)
                nc.gpsimd.memset(half_pow[:, :], -0.5).then_inc(pool_const, 1)
                pool.wait_ge(pool_const, 6)
                nc.gpsimd.affine_select(out=ident[:, :], in_=ident[:, :], compare_op=ALU.not_equal, fill=1.0,
                                        base=0, pattern=[[-1, P]], channel_multiplier=1).then_inc(pool_const, 1)
                nc.gpsimd.affine_select(out=before[:, :], in_=before[:, :], compare_op=ALU.is_ge, fill=1.0,
                                        base=0, pattern=[[-1, P]], channel_multiplier=1).then_inc(pool_const, 1)
                nc.gpsimd.iota(expert_ids[:, :], pattern=[[1, EXPERTS]], base=0, channel_multiplier=0,
                               allow_small_or_imprecise_dtypes=True).then_inc(pool_const, 1)
                nc.gpsimd.iota(list_base[:, :, :], pattern=[[0, TILES], [CAPACITY, EXPERTS]], base=0,
                               channel_multiplier=0, allow_small_or_imprecise_dtypes=True).then_inc(pool_const, 1)
                nc.gpsimd.iota(tok_ids[:, :], pattern=[[P, TILES]], base=0, channel_multiplier=1,
                               allow_small_or_imprecise_dtypes=True).then_inc(pool_const, 1)

                def root(which, count, var_done, shift_done, rstd_done):
                    pool.wait_ge(var_done, count)
                    settle(pool)
                    nc.gpsimd.tensor_scalar(shifted[:, which, :], moments[:, which, :, 1], LN_EPS, 0.0,
                                            ALU.add, ALU.add).then_inc(shift_done, 1)
                    pool.wait_ge(shift_done, count)
                    nc.gpsimd.tensor_tensor(rstd[:, which, :], shifted[:, which, :], half_pow[:, :],
                                            ALU.pow).then_inc(rstd_done, 1)

                def step(n, p, inner=False):
                    q = 1 - p
                    for s in range(HEADS):
                        g = n * HEADS + s
                        if (s == 0 and has(n, inner, -1)) or (s > 0 and has(n, inner, 0)):
                            r = (s - 1) % 4
                            pool.wait_ge(inverted, g)
                            settle(pool)
                            for t in range(TILES):
                                last = nc.gpsimd.tensor_scalar(probs[:, r, t, :], probs[:, r, t, :],
                                                               row_inv[:, r, t:t + 1], 1.0, ALU.mult, ALU.mult)
                            last.then_inc(normed, 1)
                        if 1 <= s <= DC and has(n, inner, 2):
                            c = s - 1
                            b = n + 2
                            if c == 0:
                                pool.wait_ge(c_loaded[p], (n - p) * 8 + 32)
                                need(pool, v_full, TILES * (n + 1))
                                settle(pool)
                            nc.gpsimd.tensor_copy(ct[0][:, p, c, :], cin[:, p, c, :]).then_inc(ct_hi_done, 1)
                            pool.wait_ge(ct_hi_done, b * DC + c + 1)
                            nc.gpsimd.tensor_tensor(ct[1][:, p, c, :], cin[:, p, c, :],
                                                    ct[0][:, p, c, :].bitcast(F32),
                                                    ALU.subtract).then_inc(ct_split, 1)
                        if s == 6 and has(n, inner, -1):
                            root(1, n, ln2_var, ln2_shift, ln2_rstd)
                        if s == 7 and has(n, inner, 0):
                            pool.wait_ge(x_loaded[p], (n - p) * 8 + 16)
                            if is_step(n, 0):
                                pool.wait_ge(setup_loaded, 80)
                            need(pool, x2_ready, n * TILES)
                            settle(pool)
                            for t in range(TILES):
                                last = nc.gpsimd.tensor_tensor(x_bo[:, t, :], xin[:, p, t, :], bias_o[:, :], ALU.add)
                            last.then_inc(xbo_ready, 1)
                        if s == 10 and has(n, inner, 2):
                            root(0, n + 3, ln1_var, ln1_shift, ln1_rstd)
                        if s == 15 and has(n, inner, -1):
                            if is_step(n, 1):
                                pool.wait_ge(defaults_stored, 16 * (EXPERTS + 2))
                            pool.wait_ge(rec_ready, n)
                            settle(pool)
                            for t in range(TILES):
                                for k in range(TOP_K):
                                    nc.gpsimd.indirect_dma_start(
                                        out=table[:, :],
                                        out_offset=bass.IndirectOffsetOnAxis(
                                            ap=place_i[:, t, k:k + 1].bitcast(U32), axis=0),
                                        in_=rec[:, t, k, :], in_offset=None,
                                        bounds_check=EXPERTS * CAPACITY - 1,
                                        oob_is_err=False).then_inc(rec_stored, 16)

                steps(pool, step)
                pool.wait_ge(rec_stored, 16 * TILES * TOP_K * BATCH)

            @block.scalar
            def _(act):
                def step(n, p, inner=False):
                    q = 1 - p
                    heads = has(n, inner, 0)
                    proj = has(n, inner, 1)
                    tail = has(n, inner, -1)
                    if is_step(n, -2):
                        for m in range(4):
                            act.wait_ge(w_loaded, 16 * (m + 1))
                            nc.scalar.copy(w_hi[:, m, :, :], w_raw[:, :, :]).then_inc(w_hi_done, 1)

                    def attn_hi(group, slot):
                        act.wait_ge(attended, group * HPC + HPC)
                        if slot == 0:
                            need(act, wo_full, n * TILES)
                        nc.scalar.copy(at[0][:, slot, :], attn_ps[slot % 2][:, 0:SEQ]).then_inc(at_hi_done, 1)

                    for s in range(HEADS):
                        g = n * HEADS + s
                        if tail if s < LAG else heads:
                            act.wait_ge(turned, g - LAG + 1)
                            need(act, attended, g - LAG - 1)
                            r = (s - LAG) % 2
                            nc.scalar.copy(probs_t[:, r, :, :], probs_t_ps[r][:, :, :]).then_inc(turned_copied, 1)
                        if heads:
                            act.wait_ge(masked, g + 1)
                            need(act, turned, g - 3)
                            for t in range(TILES):
                                last = nc.scalar.activation(probs[:, s % 4, t, :], neg_scores[:, s % 2, t, :],
                                                            ACT.Exp, scale=-1.0, bias=low[:, s % 4, t:t + 1],
                                                            accum_out=row_sum[:, s % 4, t:t + 1])
                            last.then_inc(exped, 1)
                        if s == 0 and proj:
                            need(act, q_full, (n + 1) * 2)
                            for t in range(TILES):
                                act.wait_ge(xt_full, (n + 1) * TILES + t + 1)
                                bank = (bank_a, bank_b)[t]
                                nc.scalar.copy(xt[0][:, :, t * P:(t + 1) * P],
                                               bank[:, :].rearrange("p (c i) -> p c i", c=DC)).then_inc(xt_hi_done, 1)
                        for which, full, ready, dst, scale, at_slots in (
                                (1, k_full, k_ready, kt, 1.0, (1, 3)), (0, q_full, q_ready, qt, -SCALE, (7, 9))):
                            if s in at_slots and proj:
                                half = at_slots.index(s)
                                act.wait_ge(full, (n + 1) * 2 + half + 1)
                                if half == 0:
                                    need(act, scored, n * HEADS)
                                if is_step(n, -1):
                                    act.wait_ge(dve_const, 4)
                                    act.wait_ge(setup_loaded, 80)
                                bank = (bank_a, bank_b)[half]
                                for i in range(2):
                                    m = half * 2 + i
                                    nc.scalar.activation(dst[:, q, m, :], bank[:, i * SEQ:(i + 1) * SEQ],
                                                         ACT.Identity, scale=scale,
                                                         bias=bias_qk[:, which, m:m + 1]).then_inc(ready, 1)
                        if s == LAG and tail:
                            attn_hi(n * DC - 1, DC - 1)
                        if s > LAG and (s - LAG) % HPC == 0 and heads:
                            attn_hi(n * DC + (s - LAG) // HPC - 1, (s - LAG) // HPC - 1)
                        if s == 10 and tail:
                            need(act, logits_full, n - 1)
                            for t in range(TILES):
                                act.wait_ge(x2t_full, n * TILES - TILES + t + 1)
                                bank = (bank_a, bank_b)[t]
                                nc.scalar.copy(x2t[:, :, t * P:(t + 1) * P],
                                               bank[:, :].rearrange("p (c i) -> p c i", c=DC)).then_inc(x2t_ready, 1)
                        if s == 13 and tail:
                            act.wait_ge(fall_ready, n)
                            nc.scalar.activation(weight_exp[:, :, :], fall[:, :, :], ACT.Exp).then_inc(weight_exped, 1)
                steps(act, step)

            @block.vector
            def _(dve):
                nc.vector.memset(ones[:, :], 1.0).then_inc(dve_const, 1)
                nc.vector.memset(members_before[:, :], 0.0).then_inc(dve_const, 1)
                dve.wait_ge(setup_loaded, 80)
                nc.vector.tensor_copy(mask_add[:, :, :], mask_u8[:, :, :]).then_inc(dve_const, 1)
                nc.vector.tensor_scalar(bias_qk[:, 0, :], bias_qk[:, 0, :], -SCALE, None, ALU.mult).then_inc(dve_const, 1)
                dve.wait_ge(dve_const, 4)
                nc.vector.tensor_reduce(row_any[:, :], mask_add[:, :, :], X_AXIS, ALU.max).then_inc(dve_const, 1)
                dve.wait_ge(dve_const, 5)
                nc.vector.tensor_scalar(mask_add[:, :, :], mask_add[:, :, :], -MASKED, MASKED, ALU.mult,
                                        ALU.add).then_inc(dve_const, 1)
                dve.wait_ge(dve_const, 6)
                dve.wait_ge(pool_const, 11)

                ROUTE = 16
                LN = 4

                def moments_of(which, chain, base, source, var_done):
                    for t in range(TILES):
                        nc.vector.bn_stats(stats[:, which, t, :], source[:, t, :]).then_inc(chain, 1)
                    dve.wait_ge(chain, base + TILES)
                    settle(dve)
                    for t in range(TILES):
                        last = nc.vector.bn_aggr(moments[:, which, t, :], stats[:, which, t, :])
                    last.then_inc(var_done, 1)

                def normalise(which, source, dst, done):
                    for t in range(TILES):
                        last = nc.vector.tensor_scalar(dst[:, t, :], source[:, t, :], moments[:, which, t, 0:1],
                                                       rstd[:, which, t:t + 1], ALU.subtract, ALU.mult)
                    last.then_inc(done, 1)

                def step(n, p, inner=False):
                    q = 1 - p
                    heads = has(n, inner, 0)
                    proj = has(n, inner, 1)
                    tail = has(n, inner, -1)
                    if is_step(n, -2):
                        for m in range(4):
                            dve.wait_ge(w_hi_done, m + 1)
                            nc.vector.tensor_tensor(w_lo[:, m, :, :], w_raw[:, :, :], w_hi[:, m, :, :].bitcast(F32),
                                                    ALU.subtract).then_inc(w_split, 1)

                    def attn_lo(group, slot):
                        dve.wait_ge(at_hi_done, group + 1)
                        nc.vector.tensor_tensor(at[1][:, slot, :], attn_ps[slot % 2][:, 0:SEQ],
                                                at[0][:, slot, :].bitcast(F32), ALU.subtract).then_inc(at_split, 1)

                    for s in range(HEADS):
                        g = n * HEADS + s
                        if heads:
                            dve.wait_ge(scored, g + 1)
                            need(dve, exped, g - 1)
                            settle(dve)
                            for t in range(TILES):
                                last = nc.vector.tensor_tensor_reduce(
                                    out=neg_scores[:, s % 2, t, :], in0=scores_ps[s % 2][:, t, :],
                                    in1=mask_add[:, t, :], scale=row_any[:, t:t + 1], scalar=3e38,
                                    op0=ALU.add, op1=ALU.min, accum_out=low[:, s % 4, t:t + 1])
                            last.then_inc(masked, 1)
                        if (s == 0 and tail) or (s > 0 and heads):
                            r = (s - 1) % 4
                            dve.wait_ge(exped, g)
                            need(dve, normed, g - 4)
                            nc.vector.reciprocal(row_inv[:, r, :], row_sum[:, r, :]).then_inc(inverted, 1)
                        if s == 0 and proj:
                            for t in range(TILES):
                                dve.wait_ge(xt_hi_done, (n + 1) * TILES + t + 1)
                                bank = (bank_a, bank_b)[t]
                                nc.vector.tensor_tensor(xt[1][:, :, t * P:(t + 1) * P],
                                                        bank[:, :].rearrange("p (c i) -> p c i", c=DC),
                                                        xt[0][:, :, t * P:(t + 1) * P].bitcast(F32),
                                                        ALU.subtract).then_inc(xt_split, 1)
                        if s == LAG and tail:
                            attn_lo(n * DC - 1, DC - 1)
                        if s > LAG and (s - LAG) % HPC == 0 and heads:
                            attn_lo(n * DC + (s - LAG) // HPC - 1, (s - LAG) // HPC - 1)
                        if s in (4, 5) and tail:
                            t = s - 4
                            dve.wait_ge(wo_full, n * TILES - TILES + t + 1)
                            if t == 0:
                                dve.wait_ge(xbo_ready, n)
                                need(dve, x2_stored, (n - 1) * 16)
                            nc.vector.tensor_tensor(x2[:, t, :], (bank_a, bank_b)[t][:, :], x_bo[:, t, :],
                                                    ALU.add).then_inc(x2_ready, 1)
                        if s == 5 and tail:
                            dve.wait_ge(x2_ready, n * TILES)
                            settle(dve)
                            need(dve, xn2_ready, n - 1)
                            moments_of(1, ln2_step, (n - 1) * TILES, x2, ln2_var)
                        if s == 7 and tail:
                            dve.wait_ge(ln2_rstd, n)
                            need(dve, xn2_stored, (n - 1) * 16)
                            need(dve, x2t_full, (n - 1) * TILES)
                            normalise(1, x2, xn2, xn2_ready)
                        if s == 9 and has(n, inner, 2):
                            dve.wait_ge(x_loaded[p], (n - p) * 8 + 32)
                            settle(dve)
                            need(dve, xn_ready, n + 2)
                            moments_of(0, ln1_step, (n + 2) * TILES, xin[:, p], ln1_var)
                        if s == 11 and has(n, inner, 2):
                            dve.wait_ge(ln1_rstd, n + 3)
                            need(dve, xt_full, (n + 2) * TILES)
                            normalise(0, xin[:, p], xn, xn_ready)
                        if s in (11, 13) and proj:
                            t = (s - 11) // 2
                            dve.wait_ge(v_full, (n + 1) * TILES + t + 1)
                            if t == 0:
                                need(dve, attended, n * HEADS)
                            nc.vector.tensor_tensor(v[:, q, t, :], bank_a[:, :], bias_v[:, :],
                                                    ALU.add).then_inc(v_ready, 1)
                        if s == 12 and tail:
                            base = (n - 1) * ROUTE
                            dve.wait_ge(logits_full, n)
                            need(dve, rec_stored, (n - 1) * 16 * TILES * TOP_K)
                            need(dve, route_step, base)
                            need(dve, rec_ready, n - 1)
                            nc.vector.tensor_copy(logits[:, :, :], bank_b[:, 0:TILES * EXPERTS].rearrange(
                                "p (t e) -> p t e", e=EXPERTS)).then_inc(logits_copied, 1)
                            dve.wait_ge(logits_copied, n)
                            settle(dve)
                            for t in range(TILES):
                                nc.vector.max(top[:, t, :], logits[:, t, :]).then_inc(route_step, 1)
                            dve.wait_ge(route_step, base + 2)
                            settle(dve)
                            for t in range(TILES):
                                nc.vector.max_index(top_at[:, t, :], top[:, t, :],
                                                    logits[:, t, :]).then_inc(route_step, 1)
                            nc.vector.tensor_tensor(fall[:, :, :], top[:, :, :],
                                                    top[:, :, 0:1].to_broadcast([P, TILES, 8]),
                                                    ALU.subtract).then_inc(fall_ready, 1)
                            dve.wait_ge(route_step, base + 4)
                            nc.vector.tensor_copy(top_id[:, :, :], top_at[:, :, 0:TOP_K]).then_inc(route_step, 1)
                            dve.wait_ge(route_step, base + 5)
                            for k in range(TOP_K):
                                nc.vector.tensor_tensor(
                                    chosen[:, :, k, :],
                                    expert_ids[:, None, :].to_broadcast([P, TILES, EXPERTS]),
                                    top_id[:, :, k:k + 1].to_broadcast([P, TILES, EXPERTS]),
                                    ALU.is_equal).then_inc(route_step, 1)
                            dve.wait_ge(route_step, base + 7)
                            nc.vector.tensor_tensor(member[:, :, :], chosen[:, :, 0, :], chosen[:, :, 1, :],
                                                    ALU.add).then_inc(member_ready, 1)
                        if s == 13 and tail:
                            base = (n - 1) * ROUTE + 7
                            dve.wait_ge(weight_exped, n)
                            nc.vector.tensor_reduce(weight_sum[:, :], weight_exp[:, :, :], X_AXIS,
                                                    ALU.add).then_inc(route_step, 1)
                            dve.wait_ge(route_step, base + 1)
                            nc.vector.reciprocal(weight_inv[:, :], weight_sum[:, :]).then_inc(route_step, 1)
                            dve.wait_ge(route_step, base + 2)
                            nc.vector.tensor_tensor(rec[:, :, :, 1].bitcast(F32), weight_exp[:, :, 0:TOP_K],
                                                    weight_inv[:, :, None].to_broadcast([P, TILES, TOP_K]),
                                                    ALU.mult).then_inc(route_step, 1)
                            nc.vector.tensor_copy(rec[:, :, :, 0], tok_ids[:, :, None].to_broadcast(
                                [P, TILES, TOP_K])).then_inc(route_step, 1)
                            dve.wait_ge(route_step, base + 4)
                            nc.vector.tensor_scalar(tok_ids[:, :], tok_ids[:, :], float(SEQ), None,
                                                    ALU.add).then_inc(route_step, 1)
                        if s == 14 and tail:
                            base = (n - 1) * ROUTE + 12
                            dve.wait_ge(place_full, n)
                            places = bank_b[:, 0:TILES * EXPERTS].rearrange("p (t e) -> p t e", e=EXPERTS)
                            nc.vector.tensor_scalar(over[:, :, :], places, float(CAPACITY), OVER, ALU.is_ge,
                                                    ALU.mult).then_inc(route_step, 1)
                            nc.vector.tensor_tensor(place[:, :, :], places, list_base[:, :, :],
                                                    ALU.add).then_inc(place_used, 1)
                            for t in range(TILES):
                                if t:
                                    dve.wait_ge(route_step, base + 2)
                                nc.vector.tensor_tensor(members_before[:, :], members_before[:, :], member[:, t, :],
                                                        ALU.add).then_inc(route_step, 1)
                            dve.wait_ge(place_used, n)
                            nc.vector.tensor_tensor(place[:, :, :], place[:, :, :], over[:, :, :],
                                                    ALU.add).then_inc(route_step, 1)
                            dve.wait_ge(route_step, base + 4)
                            for k in range(TOP_K):
                                last = nc.vector.tensor_tensor(place_k[:, :, k, :], chosen[:, :, k, :], place[:, :, :],
                                                               ALU.mult)
                            last.then_inc(place_step, 1)
                            dve.wait_ge(place_step, n * 2 - 1)
                            nc.vector.tensor_reduce(place_f[:, :, :], place_k[:, :, :, :], X_AXIS,
                                                    ALU.add).then_inc(place_step, 1)
                            dve.wait_ge(place_step, n * 2)
                            nc.vector.tensor_copy(place_i[:, :, :], place_f[:, :, :]).then_inc(rec_ready, 1)
                steps(dve, step)

            @block.tensor
            def _(pe):
                pe.wait_ge(pool_const, 11)
                pe.wait_ge(dve_const, 6)
                pe.wait_ge(setup_loaded, 80)

                def transposed(bank, source, t, done):
                    for c in range(DC):
                        last = nc.tensor.transpose(bank[:, c * P:(c + 1) * P], source[:, t, c * P:(c + 1) * P],
                                                   ident[:, :])
                    last.then_inc(done, 1)

                def columns(bank, i, m, matrix, rhs):
                    first = True
                    for c in range(DC):
                        for a, b in PASSES:
                            last = nc.tensor.matmul(bank[:, i * SEQ:(i + 1) * SEQ],
                                                    w_parts[a][:, matrix, c, m * P:(m + 1) * P], rhs[b][:, c, :],
                                                    start=first, stop=(c == DC - 1 and (a, b) == PASSES[-1]))
                            first = False
                    return last

                def rows(bank, matrix, lhs, t, done):
                    first = True
                    for c in range(DC):
                        for a, b in PASSES:
                            last = nc.tensor.matmul(bank[:, :], lhs[a][:, c, t * P:(t + 1) * P],
                                                    w_parts[b][:, matrix, c, :],
                                                    start=first, stop=(c == DC - 1 and (a, b) == PASSES[-1]))
                            first = False
                    last.then_inc(done, 1)

                def step(n, p, inner=False):
                    q = 1 - p
                    heads = has(n, inner, 0)
                    proj = has(n, inner, 1)
                    tail = has(n, inner, -1)
                    xt_rhs = [part[:, :, :] for part in xt]
                    ct_rhs = [part[:, q, :, :] for part in ct]
                    for s in range(HEADS):
                        g = n * HEADS + s
                        if heads:
                            if s == 0:
                                pe.wait_ge(q_ready, n * DC + DC)
                                pe.wait_ge(k_ready, n * DC + DC)
                            need(pe, masked, g - 1)
                            c, r = s // HPC, (s % HPC) * DK
                            for t in range(TILES):
                                last = nc.tensor.matmul(scores_ps[s % 2][:, t, :],
                                                        qt[r:r + DK, p, c, t * P:(t + 1) * P],
                                                        kt[r:r + DK, p, c, :], start=True, stop=True)
                            last.then_inc(scored, 1)
                        if tail if s < LAG else heads:
                            pe.wait_ge(normed, g - LAG + 1)
                            need(pe, turned_copied, g - LAG - 1)
                            h = (s - LAG) % HEADS
                            for u in range(TILES):
                                for t in range(TILES):
                                    last = nc.tensor.transpose(probs_t_ps[h % 2][:, u, t * P:(t + 1) * P],
                                                               probs[:, h % 4, t, u * P:(u + 1) * P],
                                                               ident[:, :])
                            last.then_inc(turned, 1)
                        if tail if s <= LAG else heads:
                            h = (s - LAG - 1) % HEADS
                            par, of = (p, n) if s > LAG else (q, n - 1)
                            c, r = h // HPC, (h % HPC) * DK
                            pe.wait_ge(turned_copied, g - LAG)
                            if h % HPC == 0:
                                need(pe, at_split, of * DC + c - 1)
                            if h == 0:
                                pe.wait_ge(v_ready, of * TILES + TILES)
                            for u in range(TILES):
                                last = nc.tensor.matmul(attn_ps[c % 2][r:r + DK, 0:SEQ],
                                                        v[:, par, u, h * DK:(h + 1) * DK],
                                                        probs_t[:, h % 2, u, :],
                                                        start=(u == 0), stop=(u == TILES - 1))
                            last.then_inc(attended, 1)

                        if s == 0 and proj:
                            pe.wait_ge(xn_ready, n + 2)
                            need(pe, v_ready, (n + 1) * TILES)
                            transposed(bank_a, xn, 0, xt_full)
                            need(pe, place_used, n - 1)
                            transposed(bank_b, xn, 1, xt_full)
                        if s in (1, 2, 3) and proj:
                            if s == 1:
                                if is_step(n, -1):
                                    pe.wait_ge(w_split, 4)
                                pe.wait_ge(ct_split, (n + 2) * DC)
                                pe.wait_ge(xt_split, (n + 1) * TILES + 1)
                                columns(bank_a, 0, 0, 1, ct_rhs)
                                columns(bank_a, 1, 1, 1, ct_rhs).then_inc(k_full, 1)
                            if s == 2:
                                pe.wait_ge(xt_split, (n + 1) * TILES + 2)
                                columns(bank_b, 0, 2, 1, ct_rhs)
                            if s == 3:
                                columns(bank_b, 1, 3, 1, ct_rhs).then_inc(k_full, 1)
                        if s in (4, 5) and tail:
                            t = s - 4
                            if t == 0:
                                pe.wait_ge(at_split, n * DC)
                            if proj:
                                pe.wait_ge(k_ready, (n + 1) * DC + 2 * (t + 1))
                            elif t == 0:
                                pe.wait_ge(v_ready, BATCH * TILES)
                                pe.wait_ge(x2t_ready, (n - 1) * TILES)
                            else:
                                pe.wait_ge(place_used, n - 1)
                            rows((bank_a, bank_b)[t], 3, at, t, wo_full)
                        if s in (6, 7, 8, 9) and proj:
                            m = s - 6
                            if m % 2 == 0:
                                if tail:
                                    pe.wait_ge(x2_ready, (n - 1) * TILES + m // 2 + 1)
                                else:
                                    pe.wait_ge(k_ready, (n + 1) * DC + m + 2)
                            last = columns((bank_a, bank_b)[m // 2], m % 2, m, 0, xt_rhs)
                            if m % 2:
                                last.then_inc(q_full, 1)
                        if s == 10 and tail:
                            pe.wait_ge(xn2_ready, n)
                            for t in range(TILES):
                                if proj:
                                    pe.wait_ge(q_ready, (n + 1) * DC + 2 * (t + 1))
                                else:
                                    pe.wait_ge(x2_ready, (n - 1) * TILES + t + 1)
                                transposed((bank_a, bank_b)[t], xn2, t, x2t_full)
                        if s in (11, 13) and proj:
                            t = (s - 11) // 2
                            if t:
                                pe.wait_ge(v_ready, (n + 1) * TILES + 1)
                            elif tail:
                                pe.wait_ge(x2t_ready, (n - 1) * TILES + 1)
                            else:
                                pe.wait_ge(q_ready, (n + 1) * DC + 2)
                            rows(bank_a, 2, [part[:, q] for part in ct], t, v_full)
                        if s == 12 and tail:
                            pe.wait_ge(x2t_ready, n * TILES)
                            for t in range(TILES):
                                for c in range(DC):
                                    last = nc.tensor.matmul(bank_b[:, t * EXPERTS:(t + 1) * EXPERTS],
                                                            x2t[:, c, t * P:(t + 1) * P], wg[:, c, :],
                                                            start=(c == 0), stop=(c == DC - 1))
                            last.then_inc(logits_full, 1)
                        if s == 14 and tail:
                            pe.wait_ge(member_ready, n)
                            for t in range(TILES):
                                terms = [(before, member[:, t, :]), (ones, members_before[:, :])]
                                terms += [(ones, member[:, u, :]) for u in range(t)]
                                for i, (a, b) in enumerate(terms):
                                    last = nc.tensor.matmul(bank_b[:, t * EXPERTS:(t + 1) * EXPERTS], a[:, :], b,
                                                            start=(i == 0), stop=(i == len(terms) - 1))
                            last.then_inc(place_full, 1)
                steps(pe, step)


def expert_block(nc, c_fc, c_proj, out, xn2_rows, table):
    from contextlib import ExitStack
    with ExitStack() as stack:
        def sb(name, shape, dt=F32):
            return stack.enter_context(nc.sbuf_tensor(name, shape, dt))

        def ps(name, shape):
            return stack.enter_context(nc.psum_tensor(name, shape, F32))

        def sem(name):
            return stack.enter_context(nc.semaphore(name))

        ident = sb("ident2", [P, P])
        fc_raw = sb("fc_raw", [P, DC, DFF])
        fc = [sb("fc_hi", [P, DC, DFF], F32R), sb("fc_lo", [P, DC, DFF], F32R)]
        pj_raw = sb("pj_raw", [P, MC, D])
        pj = [sb("pj_hi", [P, MC, D], F32R), sb("pj_lo", [P, MC, D], F32R)]
        lists = sb("lists", [P, EXPERTS, SLOTS, 2], I32)
        gather_ids = sb("gather_ids", [P, SLOTS, 2], I32)
        recs = sb("recs", [P, SLOTS, 2], I32)
        xg = sb("xg", [P, 2, CT, D])
        xt = [sb("xe_hi", [P, 2, DC, CHUNK], F32R), sb("xe_lo", [P, 2, DC, CHUNK], F32R)]
        act_part = sb("act_part", [P, 2, CHUNK])
        hidden = sb("hidden", [P, 2, CHUNK])
        ht = [sb("ht_hi", [P, MC, CHUNK], F32R), sb("ht_lo", [P, MC, CHUNK], F32R)]
        y = sb("y", [P, CT, D])

        turn_ps = [ps(f"turn_ps{i}", [P, CHUNK]) for i in range(2)]
        a_ps = [ps(f"a_ps{i}", [P, CHUNK]) for i in range(2)]
        g_ps = [ps(f"g_ps{i}", [P, CHUNK]) for i in range(2)]
        y_ps = [ps(f"y_ps{i}", [P, D]) for i in range(2)]

        ident_ready = sem("ident_ready")
        lists_loaded = sem("lists_loaded")
        fc_loaded = sem("fc_loaded")
        pj_loaded = sem("pj_loaded")
        fc_hi_done = sem("fc_hi_done")
        fc_split = sem("fc_split")
        pj_hi_done = sem("pj_hi_done")
        pj_split = sem("pj_split")
        ids_ready = sem("ids_ready")
        recs_ready = sem("recs_ready")
        gathered = [sem(f"gathered{i}") for i in range(2)]
        turned = sem("turned2")
        xt_hi_done = sem("xe_hi_done")
        xt_split = sem("xe_split")
        up_done = sem("up_done")
        silu_done = sem("silu_done")
        gated = sem("gated")
        ht_hi_done = sem("ht_hi_done")
        ht_split = sem("ht_split")
        down_done = sem("down_done")
        y_ready = sem("y_ready")
        added = sem("added")

        def experts(eng, expert):
            expert(0, False)
            with eng.Fori(1, EXPERTS - 1) as e:
                expert(e, False)
            expert(EXPERTS - 1, True)

        with nc.Block() as block:

            @block.sync
            def _(sp):
                sp.dma_start(lists[:, :, :, :], table.rearrange("(e p s) r -> p e s r", p=P, s=SLOTS)).then_inc(
                    lists_loaded, 16)
                sp.dma_start(fc_raw[:, :, :], c_fc[0]).then_inc(fc_loaded, 16)
                sp.dma_start(pj_raw[:, :, :], c_proj[0]).then_inc(pj_loaded, 16)
                with sp.Fori(1, EXPERTS) as e:
                    sp.wait_ge(fc_split, e * MC)
                    sp.dma_start(fc_raw[:, :, :], c_fc[e]).then_inc(fc_loaded, 16)
                    sp.wait_ge(pj_split, e * MC)
                    sp.dma_start(pj_raw[:, :, :], c_proj[e]).then_inc(pj_loaded, 16)

            @block.gpsimd
            def _(pool):
                nc.gpsimd.memset(ident[:, :], 0.0).then_inc(ident_ready, 1)
                pool.wait_ge(ident_ready, 1)
                nc.gpsimd.affine_select(out=ident[:, :], in_=ident[:, :], compare_op=ALU.not_equal, fill=1.0,
                                        base=0, pattern=[[-1, P]], channel_multiplier=1).then_inc(ident_ready, 1)
                pool.wait_ge(lists_loaded, 16)

                def gather(q, i):
                    par = i % 2
                    need(pool, turned, (q - 1) * DC)
                    settle(pool)
                    for t in range(CT):
                        nc.gpsimd.indirect_dma_start(
                            out=xg[:, par, t, :], out_offset=None, in_=xn2_rows[:, :],
                            in_offset=bass.IndirectOffsetOnAxis(
                                ap=gather_ids[:, i * CT + t, 0:1].bitcast(U32), axis=0)).then_inc(gathered[par], 16)

                nc.gpsimd.tensor_copy(gather_ids[:, :, :], lists[:, 0, :, :]).then_inc(ids_ready, 1)
                pool.wait_ge(ids_ready, 1)
                gather(0, 0)

                def expert(e, final):
                    for i in range(CHUNKS):
                        q = e * CHUNKS + i
                        ahead = i < CHUNKS - 1 or not final
                        if i == CHUNKS - 1 and ahead:
                            for par in range(2):
                                pool.wait_ge(gathered[par], e * (8 * CT * CHUNKS) + 8 * CT * CHUNKS)
                            settle(pool)
                            nc.gpsimd.tensor_copy(gather_ids[:, :, :], lists[:, e + 1, :, :]).then_inc(ids_ready, 1)
                            pool.wait_ge(ids_ready, e + 2)
                            settle(pool)
                        if ahead:
                            gather(q + 1, (i + 1) % CHUNKS)
                        if i == 0:
                            need(pool, added, e * (16 * SLOTS))
                            settle(pool)
                            nc.gpsimd.tensor_copy(recs[:, :, :], lists[:, e, :, :]).then_inc(recs_ready, 1)
                            pool.wait_ge(recs_ready, e + 1)
                            settle(pool)
                        for t in range(CT):
                            need(pool, y_ready, q * CT + t + 1)
                            settle(pool)
                            need(pool, added, q * (16 * CT) + 16 * t)
                            settle(pool)
                            nc.gpsimd.indirect_dma_start(
                                out=out[:, :],
                                out_offset=bass.IndirectOffsetOnAxis(
                                    ap=recs[:, i * CT + t, 0:1].bitcast(U32), axis=0),
                                in_=y[:, t, :], in_offset=None, compute_op=ALU.add).then_inc(added, 16)
                experts(pool, expert)
                need(pool, added, 16 * EXPERTS * SLOTS)

            @block.scalar
            def _(act):
                def fc_hi(e, m):
                    act.wait_ge(fc_loaded, e * 16 + 16)
                    need(act, up_done, e * (CHUNKS * MC) + (m + 1 - MC))
                    for half in (0, GATE):
                        last = nc.scalar.copy(fc[0][:, :, half + m * P:half + (m + 1) * P],
                                              fc_raw[:, :, half + m * P:half + (m + 1) * P])
                    last.then_inc(fc_hi_done, 1)

                def pj_hi(e, k):
                    act.wait_ge(pj_loaded, e * 16 + 16)
                    need(act, down_done, e * SLOTS)
                    nc.scalar.copy(pj[0][:, k, :], pj_raw[:, k, :]).then_inc(pj_hi_done, 1)

                def turn(q, par, c):
                    need(act, up_done, (q - 1) * MC)
                    act.wait_ge(turned, q * DC + c + 1)
                    nc.scalar.copy(xt[0][:, par, c, :], turn_ps[c % 2][:, :]).then_inc(xt_hi_done, 1)

                for c in range(DC):
                    turn(0, 0, c)
                for m in range(MC):
                    fc_hi(0, m)

                def expert(e, final):
                    for i in range(CHUNKS):
                        q = e * CHUNKS + i
                        for m in range(MC):
                            if i == 0:
                                pj_hi(e, m)
                            if m >= MC - DC and (i < CHUNKS - 1 or not final):
                                turn(q + 1, (i + 1) % 2, m - (MC - DC))
                            need(act, up_done, q * MC + m + 1)
                            need(act, gated, q * MC + m - 1)
                            nc.scalar.activation(act_part[:, m % 2, :], a_ps[m % 2][:, :],
                                                 ACT.Silu).then_inc(silu_done, 1)
                            need(act, gated, q * MC + m + 1)
                            need(act, down_done, q * CT)
                            nc.scalar.copy(ht[0][:, m, :], hidden[:, m % 2, :]).then_inc(ht_hi_done, 1)
                        for t in range(CT):
                            if i == CHUNKS - 1 and not final and t < MC // 2:
                                fc_hi(e + 1, 2 * t)
                                fc_hi(e + 1, 2 * t + 1)
                            need(act, down_done, q * CT + t + 1)
                            need(act, added, q * (16 * CT))
                            act.wait_ge(recs_ready, e + 1)
                            nc.scalar.activation(y[:, t, :], y_ps[t % 2][:, :], ACT.Copy,
                                                 scale=recs[:, i * CT + t, 1:2].bitcast(F32)).then_inc(y_ready, 1)
                experts(act, expert)

            @block.vector
            def _(dve):
                def low(dst, source, hi, done):
                    nc.vector.tensor_tensor(dst, source, hi.bitcast(F32), ALU.subtract).then_inc(done, 1)

                def fc_lo(e, m):
                    dve.wait_ge(fc_hi_done, e * MC + m + 1)
                    for half in (0, GATE):
                        cols = [part[:, :, half + m * P:half + (m + 1) * P] for part in (fc[1], fc_raw, fc[0])]
                        last = nc.vector.tensor_tensor(cols[0], cols[1], cols[2].bitcast(F32), ALU.subtract)
                    last.then_inc(fc_split, 1)

                def turn(q, par, c):
                    dve.wait_ge(xt_hi_done, q * DC + c + 1)
                    low(xt[1][:, par, c, :], turn_ps[c % 2][:, :], xt[0][:, par, c, :], xt_split)

                for c in range(DC):
                    turn(0, 0, c)
                for m in range(MC):
                    fc_lo(0, m)

                def expert(e, final):
                    for i in range(CHUNKS):
                        q = e * CHUNKS + i
                        for m in range(MC):
                            if i == 0:
                                dve.wait_ge(pj_hi_done, e * MC + m + 1)
                                low(pj[1][:, m, :], pj_raw[:, m, :], pj[0][:, m, :], pj_split)
                            if m >= MC - DC and (i < CHUNKS - 1 or not final):
                                turn(q + 1, (i + 1) % 2, m - (MC - DC))
                            dve.wait_ge(silu_done, q * MC + m + 1)
                            nc.vector.tensor_tensor(hidden[:, m % 2, :], act_part[:, m % 2, :], g_ps[m % 2][:, :],
                                                    ALU.mult).then_inc(gated, 1)
                            dve.wait_ge(ht_hi_done, q * MC + m + 1)
                            low(ht[1][:, m, :], hidden[:, m % 2, :], ht[0][:, m, :], ht_split)
                        if i == CHUNKS - 1 and not final:
                            for m in range(MC):
                                fc_lo(e + 1, m)
                experts(dve, expert)

            @block.tensor
            def _(pe):
                pe.wait_ge(ident_ready, 2)

                def turn(q, e, i, c):
                    if c == 0:
                        pe.wait_ge(gathered[i % 2], e * (8 * CT * CHUNKS) + 16 * CT * (i // 2 + 1))
                    need(pe, xt_split, q * DC + c - 1)
                    for t in range(CT):
                        last = nc.tensor.transpose(turn_ps[c % 2][:, t * P:(t + 1) * P],
                                                   xg[:, i % 2, t, c * P:(c + 1) * P], ident[:, :])
                    last.then_inc(turned, 1)

                for c in range(DC):
                    turn(0, 0, 0, c)

                def expert(e, final):
                    for i in range(CHUNKS):
                        q = e * CHUNKS + i
                        need(pe, xt_split, q * DC + DC)
                        for m in range(MC):
                            if m >= MC - DC and i < CHUNKS - 1:
                                turn(q + 1, e, i + 1, m - (MC - DC))
                            elif m >= MC - DC and not final:
                                turn(q + 1, e + 1, 0, m - (MC - DC))
                            if i == 0:
                                pe.wait_ge(fc_split, e * MC + m + 1)
                            need(pe, gated, q * MC + m - 1)
                            for bank, half in ((a_ps[m % 2], 0), (g_ps[m % 2], GATE)):
                                first = True
                                for c in range(DC):
                                    for a, b in PASSES:
                                        last = nc.tensor.matmul(bank[:, :],
                                                                fc[a][:, c, half + m * P:half + (m + 1) * P],
                                                                xt[b][:, i % 2, c, :], start=first,
                                                                stop=(c == DC - 1 and (a, b) == PASSES[-1]))
                                        first = False
                            last.then_inc(up_done, 1)
                        if i == 0:
                            pe.wait_ge(pj_split, e * MC + MC)
                        for t in range(CT):
                            need(pe, y_ready, q * CT + t - 1)
                            first = True
                            for m in range(MC):
                                if t == 0:
                                    pe.wait_ge(ht_split, q * MC + m + 1)
                                for a, b in PASSES:
                                    last = nc.tensor.matmul(y_ps[t % 2][:, :], ht[a][:, m, t * P:(t + 1) * P],
                                                            pj[b][:, m, :], start=first,
                                                            stop=(m == MC - 1 and (a, b) == PASSES[-1]))
                                    first = False
                            last.then_inc(down_done, 1)
                experts(pe, expert)


def build(nc, x, ctx_t, mask, w_attn, b_qk, b_v, b_o, w_gate, c_fc, c_proj, out):
    xn2_rows = nc.dram_tensor("xn2_rows", [TOKENS + P, D], F32, kind="Internal").ap()
    table = nc.dram_tensor("table", [EXPERTS * CAPACITY, 2], I32, kind="Internal").ap()
    attention_block(nc, x, ctx_t, mask, w_attn, b_qk, b_v, b_o, w_gate, out, xn2_rows, table)
    expert_block(nc, c_fc, c_proj, out, xn2_rows, table)


def kernel(**inputs):
    import numpy as np
    import concourse.bacc as bacc
    from concourse.bass_utils import run_bass_kernel_spmd

    def rows_to_partitions(a, chunks):
        a = a.reshape(a.shape[:-2] + (chunks, P, a.shape[-1]))
        return np.ascontiguousarray(np.swapaxes(a, -3, -2))

    got = {k: np.asarray(a) for k, a in inputs.items()}
    w = "L0_xattn_w"
    arrays = {
        "x": np.ascontiguousarray(got["x"].reshape(TOKENS, D)),
        "ctx_t": rows_to_partitions(np.swapaxes(got["ctx_1024"], 1, 2), DC),
        "mask": np.ascontiguousarray(got["mask_SxS2_bk0"]),
        "w_attn": rows_to_partitions(np.stack([got[w + n].T for n in "qkvo"]), DC),
        "b_qk": np.ascontiguousarray(np.stack([got["L0_xattn_bq"], got["L0_xattn_bk"]]).reshape(2, DC, P)
                                     .transpose(2, 0, 1)),
        "b_v": np.ascontiguousarray(np.broadcast_to(got["L0_xattn_bv"], (P, D))),
        "b_o": np.ascontiguousarray(np.broadcast_to(got["L0_xattn_bo"], (P, D))),
        "w_gate": rows_to_partitions(got["L0_ffn_w_gate"], DC),
        "c_fc": rows_to_partitions(got["L0_ffn_c_fc"], DC),
        "c_proj": rows_to_partitions(got["L0_ffn_c_proj"], MC),
    }
    nc = bacc.Bacc("TRN2", target_bir_lowering=False, num_devices=1)
    args = [nc.dram_tensor(f"in_{n}", a.shape, mybir.dt.from_np(a.dtype), kind="ExternalInput").ap()
            for n, a in arrays.items()]
    out = nc.dram_tensor("out", [TOKENS + P, D], F32, kind="ExternalOutput").ap()
    build(nc, *args, out)
    r = run_bass_kernel_spmd(nc, [{f"in_{n}": a for n, a in arrays.items()}], core_ids=[0])
    return r.results[0]["out"][:TOKENS].reshape(BATCH, SEQ, D)
```

```python
import concourse.bass as bass
from concourse import mybir

F32 = mybir.dt.float32
F32R = mybir.dt.float32r
BF16 = mybir.dt.bfloat16
I32 = mybir.dt.int32
U32 = mybir.dt.uint32
U8 = mybir.dt.uint8
ALU = mybir.AluOpType
ACT = mybir.ActivationFunctionType
X_AXIS = mybir.AxisListType.X

P = 128
BATCH, SEQ, D = 32, 256, 512
HEADS, DK = 16, 32
TILES = SEQ // P
DC = D // P
HPC = P // DK
TOKENS = BATCH * SEQ
EXPERTS, TOP_K, CAPACITY = 8, 2, 2048
DFF = 3 * D
GATE = DFF // 2
MC = GATE // P
SLOTS = CAPACITY // P
CHUNK = 512
CT = CHUNK // P
CHUNKS = CAPACITY // CHUNK
PIECE = 2
PIECES = MC // PIECE
LN_EPS = 1e-5
MASKED = 1e9
OVER = float(1 << 20)
SCALE = float(DK) ** -0.5
LAG = 3
PASSES = ((0, 0), (0, 1), (1, 0))
HALVES = 2
STACKED = 16 * len(PASSES) * HPC
W_ORDER = (1, 0, 2, 3)


def need(eng, sem, value):
    if isinstance(value, int) and value <= 0:
        return
    eng.wait_ge(sem, value)


def is_step(n, number):
    return isinstance(n, int) and n == number


def settle(eng):
    eng.nop(nofuse=True)


def attention_block(nc, x, ctx_t, mask, w_attn, b_qk, b_v, b_o, w_gate, out, xn2_rows, table):
    from contextlib import ExitStack
    x_rows = x.rearrange("(b t p) d -> b p t d", t=TILES, p=P)
    out_rows = out[0:TOKENS, :].rearrange("(b t p) d -> b p t d", t=TILES, p=P)
    xn2_out = xn2_rows[0:TOKENS, :].rearrange("(b t p) d -> b p t d", t=TILES, p=P)
    with ExitStack() as stack:
        def sb(name, shape, dt=F32):
            return stack.enter_context(nc.sbuf_tensor(name, shape, dt))

        def ps(name, shape):
            return stack.enter_context(nc.psum_tensor(name, shape, F32))

        def sem(name):
            return stack.enter_context(nc.semaphore(name))

        w_hi = sb("w_hi", [P, 4, DC, D], F32R)
        w_lo = sb("w_lo", [P, 4, DC, D], F32R)
        w_parts = (w_hi, w_lo)
        wg = sb("wg", [P, DC, EXPERTS])
        bias_qk = sb("bias_qk", [P, 2, DC])
        bias_v = sb("bias_v", [P, D])
        bias_o = sb("bias_o", [P, D])
        mask_u8 = sb("mask_u8", [P, TILES, SEQ], U8)
        mask_add = sb("mask_add", [P, TILES, SEQ])
        row_any = sb("row_any", [P, TILES])
        ident = sb("ident", [P, P])
        before = sb("before", [P, P], BF16)
        ones = sb("ones", [P, P], BF16)
        expert_ids = sb("expert_ids", [P, EXPERTS])
        list_base = sb("list_base", [P, TILES, EXPERTS])
        half_pow = sb("half_pow", [P, TILES])
        tok_ids = sb("tok_ids", [P, TILES])
        default_rec = sb("default_rec", [P, SLOTS, 2], I32)

        xin = sb("xin", [P, 2, TILES, D])
        xn = sb("xn", [P, TILES, D])
        xt = [sb("xt_hi", [P, DC, SEQ], F32R), sb("xt_lo", [P, DC, SEQ], F32R)]
        x_bo = sb("x_bo", [P, TILES, D])
        zeros = x_bo[:, 0, :]
        cin = sb("cin", [P, DC, SEQ])
        ct = [sb("ct_hi", [P, 2, DC, SEQ], F32R), sb("ct_lo", [P, 2, DC, SEQ], F32R)]
        qk = [sb("qk_hi", [P, 2, DC, SEQ], F32R), sb("qk_lo", [P, 2, DC, SEQ], F32R)]
        stacks = [sb(f"{name}_stack", [len(PASSES) * DK, DC, HPC, SEQ], F32R) for name in "qk"]
        v = sb("v", [P, 2, TILES, D])
        scores_sb = sb("scores_sb", [P, 4, TILES, SEQ])
        neg_scores = scores_sb[:, 0:2]
        probs_t = scores_sb[:, 2:4]
        probs = sb("probs", [P, 4, TILES, SEQ])
        low = sb("low", [P, 4, TILES])
        row_sum = sb("row_sum", [P, 4, TILES])
        row_inv = sb("row_inv", [P, 4, TILES])
        at = [sb("at_hi", [P, DC, SEQ], F32R), sb("at_lo", [P, DC, SEQ], F32R)]
        x2_xn2 = sb("x2_xn2", [P, 2, TILES, D])
        x2, xn2 = x2_xn2[:, 0], x2_xn2[:, 1]
        x2t = x2.rearrange("p t (c i) -> p (t c) i", i=SEQ)
        w_raw = [a.rearrange("p a t (c i) -> p (a t c) i", i=i).rearrange("p (c j) i -> p c (j i)", j=D // i)
                 for a, i in ((x2_xn2, D), (probs, SEQ), (v, D), (scores_sb, SEQ))]
        stats = sb("stats", [P, 2, TILES, 6])
        moments = sb("moments", [P, 2, TILES, 2])
        shifted = sb("shifted", [P, 2, TILES])
        rstd = sb("rstd", [P, 2, TILES])
        logits = sb("logits", [P, TILES, EXPERTS])
        top = sb("top", [P, TILES, 8])
        top_at = sb("top_at", [P, TILES, 8], U32)
        top_id = sb("top_id", [P, TILES, TOP_K])
        chosen = sb("chosen", [P, TILES, TOP_K, EXPERTS])
        member = sb("member", [P, TILES, EXPERTS], BF16)
        members_before = sb("members_before", [P, EXPERTS], BF16)
        fall = sb("fall", [P, TILES, 8])
        weight_exp = sb("weight_exp", [P, TILES, 8])
        weight_sum = sb("weight_sum", [P, TILES])
        weight_inv = sb("weight_inv", [P, TILES])
        over = sb("over", [P, TILES, EXPERTS])
        place = sb("place", [P, TILES, EXPERTS])
        place_k = sb("place_k", [P, TILES, TOP_K, EXPERTS])
        place_f = sb("place_f", [P, TILES, TOP_K])
        place_i = sb("place_i", [P, TILES, TOP_K], I32)
        rec = sb("rec", [P, TILES, TOP_K, 2], I32)

        scores_ps = [ps(f"scores_ps{i}", [P, TILES, SEQ]) for i in range(2)]
        probs_t_ps = [ps(f"probs_t_ps{i}", [P, TILES, SEQ]) for i in range(2)]
        attn_ps = [ps(f"attn_ps{i}", [P, 512]) for i in range(2)]
        bank_a = ps("bank_a", [P, 512])
        bank_b = ps("bank_b", [P, 512])

        setup_loaded = sem("setup_loaded")
        w_loaded = [sem(f"w_loaded{i}") for i in range(4)]
        w_hi_done = sem("w_hi_done")
        w_split = sem("w_split")
        pool_const = sem("pool_const")
        dve_const = sem("dve_const")
        defaults_stored = sem("defaults_stored")
        x_loaded = [sem(f"x_loaded{i}") for i in range(2)]
        c_loaded = sem("c_loaded")
        ln1_step = sem("ln1_step")
        ln1_var = sem("ln1_var")
        ln1_shift = sem("ln1_shift")
        ln1_rstd = sem("ln1_rstd")
        xn_ready = sem("xn_ready")
        xt_full = sem("xt_full")
        xt_hi_done = sem("xt_hi_done")
        xt_split = sem("xt_split")
        ct_hi_done = sem("ct_hi_done")
        ct_split = sem("ct_split")
        xbo_ready = sem("xbo_ready")
        q_full = sem("q_full")
        k_full = sem("k_full")
        v_full = sem("v_full")
        qk_hi_done = [sem(f"{name}_hi_done") for name in "qk"]
        q_ready = sem("q_ready")
        k_ready = sem("k_ready")
        stacked = [[sem(f"{name}_stacked{half}") for half in range(HALVES)] for name in "qk"]
        v_ready = sem("v_ready")
        scored = sem("scored")
        masked = sem("masked")
        exped = sem("exped")
        inverted = sem("inverted")
        normed = sem("normed")
        turned = sem("turned")
        turned_copied = sem("turned_copied")
        attended = sem("attended")
        at_hi_done = sem("at_hi_done")
        at_split = sem("at_split")
        wo_full = sem("wo_full")
        x2_ready = sem("x2_ready")
        x2_stored = sem("x2_stored")
        ln2_step = sem("ln2_step")
        ln2_var = sem("ln2_var")
        ln2_shift = sem("ln2_shift")
        ln2_rstd = sem("ln2_rstd")
        xn2_ready = sem("xn2_ready")
        xn2_stored = sem("xn2_stored")
        x2t_full = sem("x2t_full")
        x2t_ready = sem("x2t_ready")
        logits_full = sem("logits_full")
        logits_copied = sem("logits_copied")
        route_step = sem("route_step")
        member_ready = sem("member_ready")
        fall_ready = sem("fall_ready")
        weight_exped = sem("weight_exped")
        place_full = sem("place_full")
        place_used = sem("place_used")
        place_step = sem("place_step")
        rec_ready = sem("rec_ready")
        rec_stored = sem("rec_stored")

        def steps(eng, step):
            for n in range(-2, LOOPED):
                step(n, n % 2)
            with eng.Fori(LOOPED // 2, (BATCH - 3) // 2) as j:
                step(j * 2 + 1, 1, inner=True)
                step(j * 2 + 2, 0, inner=True)
            for n in range(BATCH - 3, BATCH + 1):
                step(n, n % 2)

        X, Y = 0, 1
        QK_AT = {1: (1, 0, Y), 2: (1, 1, X), 7: (0, 0, X), 9: (0, 1, Y)}

        WEIGHTS_AT = {5: 2, 6: 3}

        LOOPED = 3

        def bank_of(role, p):
            return (bank_a, bank_b)[(role + p) % 2]

        def has(n, inner, ahead):
            return inner or 0 <= n + ahead < BATCH

        def load_c(eng, n):
            need(eng, ct_split, n * DC)
            settle(eng)
            eng.dma_start(cin[:, :, :], ctx_t[n]).then_inc(c_loaded, 16)

        def load_x(eng, n, p):
            need(eng, xn_ready, n - 1)
            need(eng, xbo_ready, (n - 1) * TILES)
            settle(eng)
            eng.dma_start(xin[:, p, :, :], x_rows[n]).then_inc(x_loaded[p], 16)

        with nc.Block() as block:

            @block.sync
            def _(sp):
                def load_w(i):
                    sp.dma_start(w_raw[i], w_attn[W_ORDER[i]]).then_inc(w_loaded[i], 16)

                def stack_heads(which, n, half):
                    chunks = slice(half * DC // HALVES, (half + 1) * DC // HALVES)
                    need(sp, scored, (n - 1) * HEADS + (half + 1) * HEADS // HALVES)
                    settle(sp)
                    sp.wait_ge((q_ready, k_ready)[which], n * DC + (half + 1) * DC // HALVES)
                    for r in range(HPC):
                        for i, parts in enumerate(PASSES):
                            source = qk[parts[which]][r * DK:(r + 1) * DK, which, chunks, :]
                            sp.dma_start(stacks[which][i * DK:(i + 1) * DK, chunks, r, :].bitcast(F32),
                                         source.bitcast(F32)).then_inc(stacked[which][half], 16)

                def step(n, p, inner=False):
                    if is_step(n, -2):
                        load_x(sp, 0, 0)
                        load_c(sp, 0)
                        load_w(0)
                        sp.dma_start(wg[:, :, :], w_gate).then_inc(setup_loaded, 16)
                        sp.dma_start(bias_qk[:, :, :], b_qk).then_inc(setup_loaded, 16)
                        sp.dma_start(bias_v[:, :], b_v).then_inc(setup_loaded, 16)
                        sp.dma_start(bias_o[:, :], b_o).then_inc(setup_loaded, 16)
                        sp.dma_start(mask_u8[:, :, :], mask.rearrange("(t p) k -> p t k", p=P)).then_inc(setup_loaded, 16)
                        for i in range(1, 4):
                            load_w(i)
                        sp.wait_ge(pool_const, 8)
                        for e in range(EXPERTS):
                            sp.dma_start(table[e * CAPACITY:(e + 1) * CAPACITY, :].rearrange(
                                "(p s) r -> p s r", p=P), default_rec[:, :, :]).then_inc(defaults_stored, 16)
                        sp.dma_start(out[TOKENS:TOKENS + P, :], zeros).then_inc(defaults_stored, 16)
                        sp.dma_start(xn2_rows[TOKENS:TOKENS + P, :], zeros).then_inc(defaults_stored, 16)
                        return
                    if has(n, inner, 0):
                        stack_heads(1, n, 1)
                        stack_heads(0, n, 1)
                    if has(n, inner, 1):
                        stack_heads(1, n + 1, 0)
                        stack_heads(0, n + 1, 0)
                steps(sp, step)
                sp.wait_ge(defaults_stored, 16 * (EXPERTS + 2))
                sp.wait_ge(x2_stored, 16 * BATCH)
                sp.wait_ge(xn2_stored, 16 * BATCH)

            @block.gpsimd
            def _(pool):
                nc.gpsimd.memset(ident[:, :], 0.0).then_inc(pool_const, 1)
                nc.gpsimd.memset(before[:, :], 0.0).then_inc(pool_const, 1)
                nc.gpsimd.memset(zeros, 0.0).then_inc(pool_const, 1)
                nc.gpsimd.iota(default_rec[:, :, 0], pattern=[[0, SLOTS]], base=TOKENS,
                               channel_multiplier=1).then_inc(pool_const, 1)
                nc.gpsimd.iota(default_rec[:, :, 1], pattern=[[0, SLOTS]], base=0,
                               channel_multiplier=0).then_inc(pool_const, 1)
                nc.gpsimd.memset(half_pow[:, :], -0.5).then_inc(pool_const, 1)
                pool.wait_ge(pool_const, 6)
                nc.gpsimd.affine_select(out=ident[:, :], in_=ident[:, :], compare_op=ALU.not_equal, fill=1.0,
                                        base=0, pattern=[[-1, P]], channel_multiplier=1).then_inc(pool_const, 1)
                nc.gpsimd.affine_select(out=before[:, :], in_=before[:, :], compare_op=ALU.is_ge, fill=1.0,
                                        base=0, pattern=[[-1, P]], channel_multiplier=1).then_inc(pool_const, 1)
                nc.gpsimd.iota(expert_ids[:, :], pattern=[[1, EXPERTS]], base=0, channel_multiplier=0,
                               allow_small_or_imprecise_dtypes=True).then_inc(pool_const, 1)
                nc.gpsimd.iota(list_base[:, :, :], pattern=[[0, TILES], [CAPACITY, EXPERTS]], base=0,
                               channel_multiplier=0, allow_small_or_imprecise_dtypes=True).then_inc(pool_const, 1)
                nc.gpsimd.iota(tok_ids[:, :], pattern=[[P, TILES]], base=0, channel_multiplier=1,
                               allow_small_or_imprecise_dtypes=True).then_inc(pool_const, 1)

                def records(count, i):
                    t, k = divmod(i, TOP_K)
                    pool.wait_ge(rec_ready, count)
                    settle(pool)
                    nc.gpsimd.indirect_dma_start(
                        out=table[:, :],
                        out_offset=bass.IndirectOffsetOnAxis(ap=place_i[:, t, k:k + 1].bitcast(U32), axis=0),
                        in_=rec[:, t, k, :], in_offset=None, bounds_check=EXPERTS * CAPACITY - 1,
                        oob_is_err=False).then_inc(rec_stored, 16)

                def root(which, count, var_done, shift_done, rstd_done):
                    pool.wait_ge(var_done, count)
                    settle(pool)
                    nc.gpsimd.tensor_scalar(shifted[:, which, :], moments[:, which, :, 1], LN_EPS, 0.0,
                                            ALU.add, ALU.add).then_inc(shift_done, 1)
                    pool.wait_ge(shift_done, count)
                    nc.gpsimd.tensor_tensor(rstd[:, which, :], shifted[:, which, :], half_pow[:, :],
                                            ALU.pow).then_inc(rstd_done, 1)

                def step(n, p, inner=False):
                    q = 1 - p
                    for s in range(HEADS):
                        g = n * HEADS + s
                        if (s == 0 and has(n, inner, -1)) or (s > 0 and has(n, inner, 0)):
                            r = (s - 1) % 4
                            pool.wait_ge(inverted, g)
                            settle(pool)
                            for t in range(TILES):
                                last = nc.gpsimd.tensor_scalar(probs[:, r, t, :], probs[:, r, t, :],
                                                               row_inv[:, r, t:t + 1], 1.0, ALU.mult, ALU.mult)
                            last.then_inc(normed, 1)
                        if 9 <= s < 9 + DC and has(n, inner, 2):
                            c = s - 9
                            b = n + 2
                            if c == 0:
                                pool.wait_ge(c_loaded, n * 16 + 48)
                                need(pool, v_full, TILES * (n + 1))
                                settle(pool)
                            nc.gpsimd.tensor_scalar(ct[0][:, p, c, :], cin[:, c, :], 1.0, 1.0, ALU.mult,
                                                    ALU.mult).then_inc(ct_hi_done, 1)
                            pool.wait_ge(ct_hi_done, b * DC + c + 1)
                            nc.gpsimd.tensor_tensor(ct[1][:, p, c, :], cin[:, c, :],
                                                    ct[0][:, p, c, :].bitcast(F32),
                                                    ALU.subtract).then_inc(ct_split, 1)
                        if s == 7 and has(n, inner, -1):
                            root(1, n, ln2_var, ln2_shift, ln2_rstd)
                        if s in (6, 8) and has(n, inner, 0):
                            t = (s - 6) // 2
                            pool.wait_ge(x_loaded[p], (n - p) * 8 + 16)
                            if is_step(n, 0):
                                pool.wait_ge(setup_loaded, 80)
                                pool.wait_ge(defaults_stored, 16 * (EXPERTS + 2))
                            need(pool, x2_ready, n * TILES)
                            settle(pool)
                            nc.gpsimd.tensor_tensor(x_bo[:, t, :], xin[:, p, t, :], bias_o[:, :],
                                                    ALU.add).then_inc(xbo_ready, 1)
                        if s == (8 if is_step(n, -2) else 13) and has(n, inner, 2):
                            root(0, n + 3, ln1_var, ln1_shift, ln1_rstd)
                        if s < TILES * TOP_K and has(n, inner, -2):
                            if is_step(n, 2) and s == 0:
                                pool.wait_ge(defaults_stored, 16 * (EXPERTS + 2))
                            records(n - 1, s)

                steps(pool, step)
                for i in range(TILES * TOP_K):
                    records(BATCH, i)
                pool.wait_ge(rec_stored, 16 * TILES * TOP_K * BATCH)

            @block.scalar
            def _(act):
                def step(n, p, inner=False):
                    q = 1 - p
                    heads = has(n, inner, 0)
                    proj = has(n, inner, 1)
                    tail = has(n, inner, -1)

                    def weights_hi(i):
                        m = W_ORDER[i]
                        act.wait_ge(w_loaded[i], 16)
                        nc.scalar.activation(w_hi[:, m, :, :], w_raw[i], ACT.Copy,
                                             scale=1.0 if m else -SCALE).then_inc(w_hi_done, 1)

                    if is_step(n, -2):
                        weights_hi(0)
                        weights_hi(1)

                    def attn_hi(group, slot):
                        act.wait_ge(attended, group * HPC + HPC)
                        if slot == 0:
                            need(act, wo_full, n * TILES)
                        nc.scalar.copy(at[0][:, slot, :], attn_ps[slot % 2][:, 0:SEQ]).then_inc(at_hi_done, 1)

                    for s in range(HEADS):
                        g = n * HEADS + s
                        if tail if s < LAG else heads:
                            act.wait_ge(turned, g - LAG + 1)
                            need(act, attended, g - LAG - 1)
                            r = (s - LAG) % 2
                            nc.scalar.copy(probs_t[:, r], probs_t_ps[r][:, :, :]).then_inc(turned_copied, 1)
                        if s == 14 and tail:
                            act.wait_ge(fall_ready, n)
                            nc.scalar.activation(weight_exp[:, :, :], fall[:, :, :], ACT.Exp).then_inc(weight_exped, 1)
                        if heads:
                            act.wait_ge(masked, g + 1)
                            need(act, turned, g - 3)
                            for t in range(TILES):
                                last = nc.scalar.activation(probs[:, s % 4, t, :], neg_scores[:, s % 2, t, :],
                                                            ACT.Exp, scale=-1.0, bias=low[:, s % 4, t:t + 1],
                                                            accum_out=row_sum[:, s % 4, t:t + 1])
                            last.then_inc(exped, 1)
                        if s in (0, 3) and proj:
                            t = s // 3
                            if t == 0:
                                need(act, q_full, (n + 1) * 2)
                            act.wait_ge(xt_full, (n + 1) * TILES + t + 1)
                            nc.scalar.copy(xt[0][:, :, t * P:(t + 1) * P], bank_of((X, Y)[t], p)[:, :].rearrange(
                                "p (c i) -> p c i", c=DC)).then_inc(xt_hi_done, 1)
                        if s in QK_AT and proj:
                            which, half, role = QK_AT[s]
                            act.wait_ge((q_full, k_full)[which], (n + 1) * 2 + half + 1)
                            need(act, stacked[which][half], (n + 1) * STACKED)
                            if is_step(n, -1):
                                act.wait_ge(dve_const, 4)
                                act.wait_ge(setup_loaded, 80)
                            for i in range(2):
                                m = half * 2 + i
                                nc.scalar.activation(qk[0][:, which, m, :],
                                                     bank_of(role, p)[:, i * SEQ:(i + 1) * SEQ], ACT.Identity,
                                                     bias=bias_qk[:, which, m:m + 1]).then_inc(qk_hi_done[which], 1)
                        if is_step(n, -1) and s in WEIGHTS_AT:
                            weights_hi(WEIGHTS_AT[s])
                        if s == LAG and tail:
                            attn_hi(n * DC - 1, DC - 1)
                        if s > LAG and (s - LAG) % HPC == 0 and heads:
                            attn_hi(n * DC + (s - LAG) // HPC - 1, (s - LAG) // HPC - 1)
                        if s in (9, 11) and tail:
                            t = (s - 9) // 2
                            act.wait_ge(x2_stored, n * 16)
                            act.wait_ge(x2t_full, n * TILES - TILES + t + 1)
                            nc.scalar.copy(x2t[:, :, t * P:(t + 1) * P], bank_of(X, p)[:, :].rearrange(
                                "p (c i) -> p c i", c=DC)).then_inc(x2t_ready, 1)
                        if s == 14 and has(n, inner, 3):
                            load_c(act, n + 3)
                        if s == 6 and tail:
                            act.wait_ge(x2_ready, n * TILES)
                            settle(act)
                            act.dma_start(out_rows[n - 1], x2).then_inc(x2_stored, 16)
                        if s == 12 and tail:
                            act.wait_ge(xn2_ready, n)
                            settle(act)
                            act.dma_start(xn2_out[n - 1], xn2).then_inc(xn2_stored, 16)
                        if s == 10 and has(n, inner, 2) and not is_step(n, -2):
                            load_x(act, n + 2, p)
                steps(act, step)

            @block.vector
            def _(dve):
                nc.vector.memset(ones[:, :], 1.0).then_inc(dve_const, 1)
                nc.vector.memset(members_before[:, :], 0.0).then_inc(dve_const, 1)

                ROUTE = 16
                LN = 4

                def moments_of(which, chain, base, source, var_done):
                    for t in range(TILES):
                        nc.vector.bn_stats(stats[:, which, t, :], source[:, t, :]).then_inc(chain, 1)
                    dve.wait_ge(chain, base + TILES)
                    settle(dve)
                    for t in range(TILES):
                        last = nc.vector.bn_aggr(moments[:, which, t, :], stats[:, which, t, :])
                    last.then_inc(var_done, 1)

                def normalise(which, source, dst, done):
                    for t in range(TILES):
                        last = nc.vector.tensor_scalar(dst[:, t, :], source[:, t, :], moments[:, which, t, 0:1],
                                                       rstd[:, which, t:t + 1], ALU.subtract, ALU.mult)
                    last.then_inc(done, 1)

                def step(n, p, inner=False):
                    q = 1 - p
                    heads = has(n, inner, 0)
                    proj = has(n, inner, 1)
                    tail = has(n, inner, -1)

                    def split_w(i):
                        m = W_ORDER[i]
                        dve.wait_ge(w_hi_done, i + 1)
                        nc.vector.scalar_tensor_tensor(w_lo[:, m, :, :], w_raw[i], 1.0 if m else -SCALE,
                                                       w_hi[:, m, :, :].bitcast(F32), ALU.mult,
                                                       ALU.subtract).then_inc(w_split, 1)

                    def v_out(t):
                        dve.wait_ge(v_full, (n + 1) * TILES + t + 1)
                        if t == 0:
                            need(dve, attended, n * HEADS)
                        nc.vector.tensor_tensor(v[:, q, t, :], bank_of(Y, p)[:, :], bias_v[:, :],
                                                ALU.add).then_inc(v_ready, 1)

                    def attn_lo(group, slot):
                        dve.wait_ge(at_hi_done, group + 1)
                        nc.vector.tensor_tensor(at[1][:, slot, :], attn_ps[slot % 2][:, 0:SEQ],
                                                at[0][:, slot, :].bitcast(F32), ALU.subtract).then_inc(at_split, 1)

                    for s in range(HEADS):
                        g = n * HEADS + s
                        if heads:
                            dve.wait_ge(scored, g + 1)
                            need(dve, exped, g - 1)
                            settle(dve)
                            for t in range(TILES):
                                last = nc.vector.tensor_tensor_reduce(
                                    out=neg_scores[:, s % 2, t, :], in0=scores_ps[s % 2][:, t, :],
                                    in1=mask_add[:, t, :], scale=row_any[:, t:t + 1], scalar=3e38,
                                    op0=ALU.add, op1=ALU.min, accum_out=low[:, s % 4, t:t + 1])
                            last.then_inc(masked, 1)
                        if (s == 0 and tail) or (s > 0 and heads):
                            r = (s - 1) % 4
                            dve.wait_ge(exped, g)
                            need(dve, normed, g - 4)
                            nc.vector.reciprocal(row_inv[:, r, :], row_sum[:, r, :]).then_inc(inverted, 1)
                        if s in (1, 4) and proj:
                            t = s // 3
                            dve.wait_ge(xt_hi_done, (n + 1) * TILES + t + 1)
                            nc.vector.tensor_tensor(xt[1][:, :, t * P:(t + 1) * P],
                                                    bank_of((X, Y)[t], p)[:, :].rearrange("p (c i) -> p c i", c=DC),
                                                    xt[0][:, :, t * P:(t + 1) * P].bitcast(F32),
                                                    ALU.subtract).then_inc(xt_split, 1)
                        if s - 1 in QK_AT and proj:
                            which, half, role = QK_AT[s - 1]
                            dve.wait_ge(qk_hi_done[which], (n + 1) * DC + half * 2 + 2)
                            for i in range(2):
                                m = half * 2 + i
                                nc.vector.scalar_tensor_tensor(
                                    qk[1][:, which, m, :], bank_of(role, p)[:, i * SEQ:(i + 1) * SEQ],
                                    bias_qk[:, which, m:m + 1], qk[0][:, which, m, :].bitcast(F32), ALU.add,
                                    ALU.subtract).then_inc((q_ready, k_ready)[which], 1)
                        if s == 0 and tail:
                            attn_lo(n * DC - 2, DC - 2)
                        if is_step(n, -1) and s in WEIGHTS_AT:
                            split_w(WEIGHTS_AT[s])
                        if s == LAG and tail:
                            attn_lo(n * DC - 1, DC - 1)
                        if s > LAG + 1 and (s - LAG) % HPC == 1 and heads:
                            attn_lo(n * DC + (s - LAG) // HPC - 1, (s - LAG) // HPC - 1)
                        if s in (4, 5) and tail:
                            t = s - 4
                            dve.wait_ge(wo_full, n * TILES - TILES + t + 1)
                            if t == 0:
                                dve.wait_ge(xbo_ready, n * TILES)
                                need(dve, logits_full, n - 1)
                            nc.vector.tensor_tensor(x2[:, t, :], bank_of((X, Y)[t], p)[:, :], x_bo[:, t, :],
                                                    ALU.add).then_inc(x2_ready, 1)
                        if s == 6 and tail:
                            dve.wait_ge(x2_ready, n * TILES)
                            settle(dve)
                            need(dve, xn2_ready, n - 1)
                            moments_of(1, ln2_step, (n - 1) * TILES, x2, ln2_var)
                        if s == 8 and tail:
                            dve.wait_ge(ln2_rstd, n)
                            need(dve, xn2_stored, (n - 1) * 16)
                            need(dve, x2t_full, (n - 1) * TILES)
                            normalise(1, x2, xn2, xn2_ready)
                        if s == 12 and proj:
                            v_out(0)
                        if s == 12 and has(n, inner, 2):
                            dve.wait_ge(x_loaded[p], (n - p) * 8 + 32)
                            settle(dve)
                            need(dve, xn_ready, n + 2)
                            moments_of(0, ln1_step, (n + 2) * TILES, xin[:, p], ln1_var)
                        if s == 13 and tail:
                            base = (n - 1) * ROUTE
                            dve.wait_ge(logits_full, n)
                            need(dve, rec_stored, (n - 1) * 16 * TILES * TOP_K)
                            need(dve, route_step, base)
                            need(dve, rec_ready, n - 1)
                            nc.vector.tensor_copy(logits[:, :, :], bank_of(X, p)[:, 0:TILES * EXPERTS].rearrange(
                                "p (t e) -> p t e", e=EXPERTS)).then_inc(logits_copied, 1)
                            dve.wait_ge(logits_copied, n)
                            settle(dve)
                            for t in range(TILES):
                                nc.vector.max(top[:, t, :], logits[:, t, :]).then_inc(route_step, 1)
                            dve.wait_ge(route_step, base + 2)
                            settle(dve)
                            for t in range(TILES):
                                nc.vector.max_index(top_at[:, t, :], top[:, t, :],
                                                    logits[:, t, :]).then_inc(route_step, 1)
                            nc.vector.tensor_tensor(fall[:, :, :], top[:, :, :],
                                                    top[:, :, 0:1].to_broadcast([P, TILES, 8]),
                                                    ALU.subtract).then_inc(fall_ready, 1)
                            dve.wait_ge(route_step, base + 4)
                            nc.vector.tensor_copy(top_id[:, :, :], top_at[:, :, 0:TOP_K]).then_inc(route_step, 1)
                            dve.wait_ge(route_step, base + 5)
                            for k in range(TOP_K):
                                nc.vector.tensor_tensor(
                                    chosen[:, :, k, :],
                                    expert_ids[:, None, :].to_broadcast([P, TILES, EXPERTS]),
                                    top_id[:, :, k:k + 1].to_broadcast([P, TILES, EXPERTS]),
                                    ALU.is_equal).then_inc(route_step, 1)
                            dve.wait_ge(route_step, base + 7)
                            nc.vector.tensor_tensor(member[:, :, :], chosen[:, :, 0, :], chosen[:, :, 1, :],
                                                    ALU.add).then_inc(member_ready, 1)
                        if s == 14 and tail:
                            base = (n - 1) * ROUTE + 7
                            dve.wait_ge(weight_exped, n)
                            nc.vector.tensor_reduce(weight_sum[:, :], weight_exp[:, :, :], X_AXIS,
                                                    ALU.add).then_inc(route_step, 1)
                            dve.wait_ge(route_step, base + 1)
                            nc.vector.reciprocal(weight_inv[:, :], weight_sum[:, :]).then_inc(route_step, 1)
                            dve.wait_ge(route_step, base + 2)
                            nc.vector.tensor_tensor(rec[:, :, :, 1].bitcast(F32), weight_exp[:, :, 0:TOP_K],
                                                    weight_inv[:, :, None].to_broadcast([P, TILES, TOP_K]),
                                                    ALU.mult).then_inc(route_step, 1)
                            nc.vector.tensor_copy(rec[:, :, :, 0], tok_ids[:, :, None].to_broadcast(
                                [P, TILES, TOP_K])).then_inc(route_step, 1)
                            dve.wait_ge(route_step, base + 4)
                            nc.vector.tensor_scalar(tok_ids[:, :], tok_ids[:, :], float(SEQ), None,
                                                    ALU.add).then_inc(route_step, 1)
                        if s == 14 and has(n, inner, 2):
                            dve.wait_ge(ln1_rstd, n + 3)
                            need(dve, xt_full, (n + 2) * TILES)
                            normalise(0, xin[:, p], xn, xn_ready)
                        if s == 15 and proj:
                            v_out(1)
                        if s == 15 and tail:
                            base = (n - 1) * ROUTE + 12
                            dve.wait_ge(place_full, n)
                            places = bank_of(X, p)[:, 0:TILES * EXPERTS].rearrange("p (t e) -> p t e", e=EXPERTS)
                            nc.vector.tensor_scalar(over[:, :, :], places, float(CAPACITY), OVER, ALU.is_ge,
                                                    ALU.mult).then_inc(route_step, 1)
                            nc.vector.tensor_tensor(place[:, :, :], places, list_base[:, :, :],
                                                    ALU.add).then_inc(place_used, 1)
                            for t in range(TILES):
                                if t:
                                    dve.wait_ge(route_step, base + 2)
                                nc.vector.tensor_tensor(members_before[:, :], members_before[:, :], member[:, t, :],
                                                        ALU.add).then_inc(route_step, 1)
                            dve.wait_ge(place_used, n)
                            nc.vector.tensor_tensor(place[:, :, :], place[:, :, :], over[:, :, :],
                                                    ALU.add).then_inc(route_step, 1)
                            dve.wait_ge(route_step, base + 4)
                            for k in range(TOP_K):
                                last = nc.vector.tensor_tensor(place_k[:, :, k, :], chosen[:, :, k, :], place[:, :, :],
                                                               ALU.mult)
                            last.then_inc(place_step, 1)
                            dve.wait_ge(place_step, n * 2 - 1)
                            nc.vector.tensor_reduce(place_f[:, :, :], place_k[:, :, :, :], X_AXIS,
                                                    ALU.add).then_inc(place_step, 1)
                            dve.wait_ge(place_step, n * 2)
                            nc.vector.tensor_copy(place_i[:, :, :], place_f[:, :, :]).then_inc(rec_ready, 1)
                    if is_step(n, -2):
                        split_w(0)
                        dve.wait_ge(setup_loaded, 80)
                        nc.vector.tensor_copy(mask_add[:, :, :], mask_u8[:, :, :]).then_inc(dve_const, 1)
                        nc.vector.tensor_scalar(bias_qk[:, 0, :], bias_qk[:, 0, :], -SCALE, None, ALU.mult).then_inc(dve_const, 1)
                        dve.wait_ge(dve_const, 4)
                        nc.vector.tensor_reduce(row_any[:, :], mask_add[:, :, :], X_AXIS, ALU.max).then_inc(dve_const, 1)
                        dve.wait_ge(dve_const, 5)
                        nc.vector.tensor_scalar(mask_add[:, :, :], mask_add[:, :, :], -MASKED, MASKED, ALU.mult,
                                                ALU.add).then_inc(dve_const, 1)
                        dve.wait_ge(dve_const, 6)
                        dve.wait_ge(pool_const, 11)

                    if is_step(n, -2):
                        split_w(1)
                steps(dve, step)

            @block.tensor
            def _(pe):
                pe.wait_ge(pool_const, 11)

                def transposed(bank, source, t, done):
                    for c in range(DC):
                        last = nc.tensor.transpose(bank[:, c * P:(c + 1) * P], source[:, t, c * P:(c + 1) * P],
                                                   ident[:, :])
                    last.then_inc(done, 1)

                def columns(bank, i, m, matrix, rhs):
                    first = True
                    for c in range(DC):
                        for a, b in PASSES:
                            last = nc.tensor.matmul(bank[:, i * SEQ:(i + 1) * SEQ],
                                                    w_parts[a][:, matrix, c, m * P:(m + 1) * P], rhs[b][:, c, :],
                                                    start=first, stop=(c == DC - 1 and (a, b) == PASSES[-1]))
                            first = False
                    return last

                def rows(bank, matrix, lhs, t, done, chunks=range(DC), split=None, base=0):
                    first = chunks[0] == 0
                    for c in chunks:
                        if split is not None:
                            pe.wait_ge(split, base + c + 1)
                        for a, b in PASSES:
                            last = nc.tensor.matmul(bank[:, :], lhs[a][:, c, t * P:(t + 1) * P],
                                                    w_parts[b][:, matrix, c, :],
                                                    start=first, stop=(c == DC - 1 and (a, b) == PASSES[-1]))
                            first = False
                    if chunks[-1] == DC - 1:
                        last.then_inc(done, 1)

                def step(n, p, inner=False):
                    q = 1 - p
                    heads = has(n, inner, 0)
                    proj = has(n, inner, 1)
                    tail = has(n, inner, -1)
                    xt_rhs = [part[:, :, :] for part in xt]
                    ct_rhs = [part[:, q, :, :] for part in ct]
                    for s in range(HEADS):
                        g = n * HEADS + s
                        if heads:
                            if s % (HEADS // HALVES) == 0:
                                for which in range(2):
                                    pe.wait_ge(stacked[which][s * HALVES // HEADS], (n + 1) * STACKED)
                            need(pe, masked, g - 1)
                            for t in range(TILES):
                                last = nc.tensor.matmul(scores_ps[s % 2][:, t, :],
                                                        stacks[0][:, s // HPC, s % HPC, t * P:(t + 1) * P],
                                                        stacks[1][:, s // HPC, s % HPC, :], start=True, stop=True)
                            last.then_inc(scored, 1)
                        if tail if s < LAG else heads:
                            pe.wait_ge(normed, g - LAG + 1)
                            h = (s - LAG) % HEADS
                            for u in range(TILES):
                                for t in range(TILES):
                                    last = nc.tensor.transpose(probs_t_ps[h % 2][:, u, t * P:(t + 1) * P],
                                                               probs[:, h % 4, t, u * P:(u + 1) * P],
                                                               ident[:, :])
                            last.then_inc(turned, 1)
                        if tail if s <= LAG else heads:
                            h = (s - LAG - 1) % HEADS
                            par, of = (p, n) if s > LAG else (q, n - 1)
                            c, r = h // HPC, (h % HPC) * DK
                            pe.wait_ge(turned_copied, g - LAG)
                            if h % HPC == 0:
                                need(pe, at_split, of * DC + c - 1)
                            if h == 0:
                                pe.wait_ge(v_ready, of * TILES + TILES)
                            for u in range(TILES):
                                last = nc.tensor.matmul(attn_ps[c % 2][r:r + DK, 0:SEQ],
                                                        v[:, par, u, h * DK:(h + 1) * DK],
                                                        probs_t[:, h % 2, u, :],
                                                        start=(u == 0), stop=(u == TILES - 1))
                            last.then_inc(attended, 1)

                        if s == 0 and proj:
                            pe.wait_ge(xn_ready, n + 2)
                            need(pe, v_ready, (n + 1) * TILES)
                            transposed(bank_of(X, p), xn, 0, xt_full)
                        if s == 1 and proj:
                            if is_step(n, -1):
                                pe.wait_ge(w_split, 1)
                            pe.wait_ge(ct_split, (n + 2) * DC)
                            need(pe, q_ready, (n + 1) * DC)
                            need(pe, place_used, n - 1)
                            for i in range(2):
                                last = columns(bank_of(Y, p), i, i, 1, ct_rhs)
                            last.then_inc(k_full, 1)
                        if s == 2 and proj:
                            pe.wait_ge(xt_split, (n + 1) * TILES + 1)
                            for i in range(2):
                                last = columns(bank_of(X, p), i, 2 + i, 1, ct_rhs)
                            last.then_inc(k_full, 1)
                        if s == 3 and proj:
                            pe.wait_ge(k_ready, (n + 1) * DC + 2)
                            transposed(bank_of(Y, p), xn, 1, xt_full)
                        if s == 4 and tail:
                            if is_step(n, 1):
                                pe.wait_ge(w_split, 4)
                            if proj:
                                pe.wait_ge(k_ready, (n + 1) * DC + DC)
                            else:
                                pe.wait_ge(v_ready, BATCH * TILES)
                                need(pe, x2_ready, (n - 1) * TILES)
                            rows(bank_of(X, p), 3, at, 0, wo_full, split=at_split, base=(n - 1) * DC)
                        if s == 5 and tail:
                            if proj:
                                pe.wait_ge(xt_split, (n + 1) * TILES + 2)
                            else:
                                pe.wait_ge(place_used, n - 1)
                            rows(bank_of(Y, p), 3, at, 1, wo_full)
                        if s in (6, 7, 8, 9) and proj:
                            m = s - 6
                            if m == 0:
                                if is_step(n, -1):
                                    pe.wait_ge(w_split, 2)
                                pe.wait_ge(xt_split, (n + 1) * TILES + 2)
                            if m % 2 == 0:
                                if tail:
                                    pe.wait_ge(x2_ready, (n - 1) * TILES + m // 2 + 1)
                                elif m == 0:
                                    pe.wait_ge(k_ready, (n + 1) * DC + DC)
                            last = columns(bank_of((X, Y)[m // 2], p), m % 2, m, 0, xt_rhs)
                            if m % 2:
                                last.then_inc(q_full, 1)
                        if s == 9 and tail:
                            pe.wait_ge(xn2_ready, n)
                            if proj:
                                pe.wait_ge(q_ready, (n + 1) * DC + 2)
                            else:
                                pe.wait_ge(x2_ready, (n - 1) * TILES + 1)
                            transposed(bank_of(X, p), xn2, 0, x2t_full)
                        if s == 11 and tail:
                            pe.wait_ge(x2t_ready, (n - 1) * TILES + 1)
                            transposed(bank_of(X, p), xn2, 1, x2t_full)
                        if s == 13 and tail:
                            if is_step(n, 1):
                                pe.wait_ge(setup_loaded, 80)
                                pe.wait_ge(dve_const, 6)
                            pe.wait_ge(x2t_ready, n * TILES)
                            for t in range(TILES):
                                for c in range(DC):
                                    last = nc.tensor.matmul(bank_of(X, p)[:, t * EXPERTS:(t + 1) * EXPERTS],
                                                            x2t[:, c, t * P:(t + 1) * P], wg[:, c, :],
                                                            start=(c == 0), stop=(c == DC - 1))
                            last.then_inc(logits_full, 1)
                        if s in (11, 13, 14) and proj:
                            if is_step(n, -1) and s == 11:
                                pe.wait_ge(w_split, 3)
                            if s == 11:
                                pe.wait_ge(q_ready, (n + 1) * DC + DC)
                            if s == 13:
                                pe.wait_ge(v_ready, (n + 1) * TILES + 1)
                            rows(bank_of(Y, p), 2, [part[:, q] for part in ct], 0 if s == 11 else 1, v_full,
                                 {11: range(DC), 13: range(DC // 2), 14: range(DC // 2, DC)}[s])
                        if s == 15 and tail:
                            pe.wait_ge(member_ready, n)
                            for t in range(TILES):
                                terms = [(before, member[:, t, :]), (ones, members_before[:, :])]
                                terms += [(ones, member[:, u, :]) for u in range(t)]
                                for i, (a, b) in enumerate(terms):
                                    last = nc.tensor.matmul(bank_of(X, p)[:, t * EXPERTS:(t + 1) * EXPERTS], a[:, :],
                                                            b, start=(i == 0), stop=(i == len(terms) - 1))
                            last.then_inc(place_full, 1)
                steps(pe, step)


def expert_block(nc, c_fc, c_proj, out, xn2_rows, table):
    from contextlib import ExitStack
    with ExitStack() as stack:
        def sb(name, shape, dt=F32):
            return stack.enter_context(nc.sbuf_tensor(name, shape, dt))

        def ps(name, shape):
            return stack.enter_context(nc.psum_tensor(name, shape, F32))

        def sem(name):
            return stack.enter_context(nc.semaphore(name))

        ident = sb("ident2", [P, P])
        fc_raw = sb("fc_raw", [P, DC * 2, GATE])
        fc = [sb("fc_hi", [P, DC * 2, GATE], F32R), sb("fc_lo", [P, DC * 2, GATE], F32R)]
        pj_raw = sb("pj_raw", [P, MC, D])
        pj = [sb("pj_hi", [P, MC, D], F32R), sb("pj_lo", [P, MC, D], F32R)]
        lists = sb("lists", [P, EXPERTS, SLOTS, 2], I32)
        gather_ids = sb("gather_ids", [P, SLOTS, 2], I32)
        recs = sb("recs", [P, SLOTS, 2], I32)
        xg = sb("xg", [P, 2, CT, D])
        xt = [sb("xe_hi", [P, 2, DC, CHUNK], F32R), sb("xe_lo", [P, 2, DC, CHUNK], F32R)]
        act_part = sb("act_part", [P, 2, CHUNK])
        hidden = sb("hidden", [P, 2, CHUNK])
        ht = [sb("ht_hi", [P, MC, CHUNK], F32R), sb("ht_lo", [P, MC, CHUNK], F32R)]
        y = sb("y", [P, CT, D])

        turn_ps = [ps(f"turn_ps{i}", [P, CHUNK]) for i in range(2)]
        a_ps = [ps(f"a_ps{i}", [P, CHUNK]) for i in range(2)]
        g_ps = [ps(f"g_ps{i}", [P, CHUNK]) for i in range(2)]
        y_ps = [ps(f"y_ps{i}", [P, D]) for i in range(2)]

        ident_ready = sem("ident_ready")
        lists_loaded = sem("lists_loaded")
        fc_loaded = [sem(f"fc_loaded{j}") for j in range(PIECES)]
        pj_loaded = sem("pj_loaded")
        fc_hi_done = sem("fc_hi_done")
        fc_split = sem("fc_split")
        pj_hi_done = sem("pj_hi_done")
        pj_split = sem("pj_split")
        ids_ready = sem("ids_ready")
        recs_ready = sem("recs_ready")
        gathered = [sem(f"gathered{i}") for i in range(2)]
        turned = sem("turned2")
        xt_hi_done = sem("xe_hi_done")
        xt_split = sem("xe_split")
        up_done = sem("up_done")
        silu_done = sem("silu_done")
        gated = sem("gated")
        ht_hi_done = sem("ht_hi_done")
        ht_split = sem("ht_split")
        down_done = sem("down_done")
        y_ready = sem("y_ready")
        added = sem("added")

        def experts(eng, expert):
            expert(0, False)
            with eng.Fori(1, EXPERTS - 1) as e:
                expert(e, False)
            expert(EXPERTS - 1, True)

        with nc.Block() as block:

            @block.sync
            def _(sp):
                sp.dma_start(lists[:, :, :, :], table.rearrange("(e p s) r -> p e s r", p=P, s=SLOTS)).then_inc(
                    lists_loaded, 16)

                def load_fc(e, j):
                    cols = slice(j * PIECE * P, (j + 1) * PIECE * P)
                    sp.dma_start(fc_raw[:, :, cols], c_fc[e].rearrange(
                        "p c (h i) -> p (c h) i", h=2)[:, :, cols]).then_inc(fc_loaded[j], 16)

                load_fc(0, 0)
                sp.wait_ge(gathered[0], 16 * CT)
                for j in range(1, PIECES):
                    load_fc(0, j)
                sp.dma_start(pj_raw[:, :, :], c_proj[0]).then_inc(pj_loaded, 16)
                with sp.Fori(1, EXPERTS) as e:
                    for j in range(PIECES):
                        if j == 0:
                            sp.wait_ge(fc_split, e * MC)
                            settle(sp)
                        sp.wait_ge(up_done, e * (CHUNKS * MC) - (CHUNKS - j) * MC + MC // 2)
                        settle(sp)
                        load_fc(e, j)
                    sp.wait_ge(pj_split, e * MC)
                    settle(sp)
                    sp.wait_ge(up_done, e * (CHUNKS * MC) - MC + MC // 2)
                    settle(sp)
                    sp.dma_start(pj_raw[:, :, :], c_proj[e]).then_inc(pj_loaded, 16)

            @block.gpsimd
            def _(pool):
                nc.gpsimd.memset(ident[:, :], 0.0).then_inc(ident_ready, 1)
                pool.wait_ge(ident_ready, 1)
                nc.gpsimd.affine_select(out=ident[:, :], in_=ident[:, :], compare_op=ALU.not_equal, fill=1.0,
                                        base=0, pattern=[[-1, P]], channel_multiplier=1).then_inc(ident_ready, 1)
                pool.wait_ge(lists_loaded, 16)

                def gather(q, i):
                    par = i % 2
                    need(pool, turned, (q - 1) * DC)
                    settle(pool)
                    for t in range(CT):
                        nc.gpsimd.indirect_dma_start(
                            out=xg[:, par, t, :], out_offset=None, in_=xn2_rows[:, :],
                            in_offset=bass.IndirectOffsetOnAxis(
                                ap=gather_ids[:, i * CT + t, 0:1].bitcast(U32), axis=0)).then_inc(gathered[par], 16)

                nc.gpsimd.tensor_copy(gather_ids[:, :, :], lists[:, 0, :, :]).then_inc(ids_ready, 1)
                pool.wait_ge(ids_ready, 1)
                gather(0, 0)

                def expert(e, final):
                    for i in range(CHUNKS):
                        q = e * CHUNKS + i
                        ahead = i < CHUNKS - 1 or not final
                        if i == CHUNKS - 1 and ahead:
                            for par in range(2):
                                pool.wait_ge(gathered[par], e * (8 * CT * CHUNKS) + 8 * CT * CHUNKS)
                            settle(pool)
                            nc.gpsimd.tensor_copy(gather_ids[:, :, :], lists[:, e + 1, :, :]).then_inc(ids_ready, 1)
                            pool.wait_ge(ids_ready, e + 2)
                            settle(pool)
                        if ahead:
                            gather(q + 1, (i + 1) % CHUNKS)
                        if i == 0:
                            need(pool, added, e * (16 * SLOTS))
                            settle(pool)
                            nc.gpsimd.tensor_copy(recs[:, :, :], lists[:, e, :, :]).then_inc(recs_ready, 1)
                            pool.wait_ge(recs_ready, e + 1)
                            settle(pool)
                        for t in range(CT):
                            need(pool, y_ready, q * CT + t + 1)
                            settle(pool)
                            need(pool, added, q * (16 * CT) + 16 * t)
                            settle(pool)
                            nc.gpsimd.indirect_dma_start(
                                out=out[:, :],
                                out_offset=bass.IndirectOffsetOnAxis(
                                    ap=recs[:, i * CT + t, 0:1].bitcast(U32), axis=0),
                                in_=y[:, t, :], in_offset=None, compute_op=ALU.add).then_inc(added, 16)
                experts(pool, expert)
                need(pool, added, 16 * EXPERTS * SLOTS)

            @block.scalar
            def _(act):
                def fc_hi(e, m):
                    act.wait_ge(fc_loaded[m // PIECE], e * 16 + 16)
                    need(act, up_done, e * (CHUNKS * MC) + (m + 1 - MC))
                    cols = slice(m * P, (m + 1) * P)
                    nc.scalar.copy(fc[0][:, :, cols], fc_raw[:, :, cols]).then_inc(fc_hi_done, 1)

                def pj_hi(e, k):
                    act.wait_ge(pj_loaded, e * 16 + 16)
                    need(act, down_done, e * SLOTS)
                    nc.scalar.copy(pj[0][:, k, :], pj_raw[:, k, :]).then_inc(pj_hi_done, 1)

                def turn(q, par, c):
                    need(act, up_done, (q - 1) * MC)
                    act.wait_ge(turned, q * DC + c + 1)
                    nc.scalar.copy(xt[0][:, par, c, :], turn_ps[c % 2][:, :]).then_inc(xt_hi_done, 1)

                fc_hi(0, 0)
                for c in range(DC):
                    turn(0, 0, c)
                for m in range(1, MC):
                    fc_hi(0, m)

                def expert(e, final):
                    for i in range(CHUNKS):
                        q = e * CHUNKS + i
                        for m in range(MC):
                            if i == 0:
                                pj_hi(e, m)
                            if m >= MC - DC and (i < CHUNKS - 1 or not final):
                                turn(q + 1, (i + 1) % 2, m - (MC - DC))
                            need(act, up_done, q * MC + m + 1)
                            need(act, gated, q * MC + m - 1)
                            nc.scalar.activation(act_part[:, m % 2, :], a_ps[m % 2][:, :],
                                                 ACT.Silu).then_inc(silu_done, 1)
                            need(act, gated, q * MC + m + 1)
                            need(act, down_done, q * CT)
                            nc.scalar.copy(ht[0][:, m, :], hidden[:, m % 2, :]).then_inc(ht_hi_done, 1)
                        for t in range(CT):
                            if i == CHUNKS - 1 and not final and t < MC // 2:
                                fc_hi(e + 1, 2 * t)
                                fc_hi(e + 1, 2 * t + 1)
                            need(act, down_done, q * CT + t + 1)
                            need(act, added, q * (16 * CT))
                            act.wait_ge(recs_ready, e + 1)
                            nc.scalar.activation(y[:, t, :], y_ps[t % 2][:, :], ACT.Copy,
                                                 scale=recs[:, i * CT + t, 1:2].bitcast(F32)).then_inc(y_ready, 1)
                experts(act, expert)

            @block.vector
            def _(dve):
                def low(dst, source, hi, done):
                    nc.vector.tensor_tensor(dst, source, hi.bitcast(F32), ALU.subtract).then_inc(done, 1)

                def fc_lo(e, m):
                    dve.wait_ge(fc_hi_done, e * MC + m + 1)
                    cols = slice(m * P, (m + 1) * P)
                    low(fc[1][:, :, cols], fc_raw[:, :, cols], fc[0][:, :, cols], fc_split)

                def turn(q, par, c):
                    dve.wait_ge(xt_hi_done, q * DC + c + 1)
                    low(xt[1][:, par, c, :], turn_ps[c % 2][:, :], xt[0][:, par, c, :], xt_split)

                fc_lo(0, 0)
                for c in range(DC):
                    turn(0, 0, c)
                for m in range(1, MC):
                    fc_lo(0, m)

                def expert(e, final):
                    for i in range(CHUNKS):
                        q = e * CHUNKS + i
                        for m in range(MC):
                            if i == 0:
                                dve.wait_ge(pj_hi_done, e * MC + m + 1)
                                low(pj[1][:, m, :], pj_raw[:, m, :], pj[0][:, m, :], pj_split)
                            if m >= MC - DC and (i < CHUNKS - 1 or not final):
                                turn(q + 1, (i + 1) % 2, m - (MC - DC))
                            dve.wait_ge(silu_done, q * MC + m + 1)
                            nc.vector.tensor_tensor(hidden[:, m % 2, :], act_part[:, m % 2, :], g_ps[m % 2][:, :],
                                                    ALU.mult).then_inc(gated, 1)
                            dve.wait_ge(ht_hi_done, q * MC + m + 1)
                            low(ht[1][:, m, :], hidden[:, m % 2, :], ht[0][:, m, :], ht_split)
                        if i == CHUNKS - 1 and not final:
                            for m in range(MC):
                                fc_lo(e + 1, m)
                experts(dve, expert)

            @block.tensor
            def _(pe):
                pe.wait_ge(ident_ready, 2)

                def turn(q, e, i, c):
                    if c == 0:
                        pe.wait_ge(gathered[i % 2], e * (8 * CT * CHUNKS) + 16 * CT * (i // 2 + 1))
                    need(pe, xt_split, q * DC + c - 1)
                    for t in range(CT):
                        last = nc.tensor.transpose(turn_ps[c % 2][:, t * P:(t + 1) * P],
                                                   xg[:, i % 2, t, c * P:(c + 1) * P], ident[:, :])
                    last.then_inc(turned, 1)

                for c in range(DC):
                    turn(0, 0, 0, c)

                def expert(e, final):
                    for i in range(CHUNKS):
                        q = e * CHUNKS + i
                        need(pe, xt_split, q * DC + DC)
                        for m in range(MC):
                            if m >= MC - DC and i < CHUNKS - 1:
                                turn(q + 1, e, i + 1, m - (MC - DC))
                            elif m >= MC - DC and not final:
                                turn(q + 1, e + 1, 0, m - (MC - DC))
                            if i == 0:
                                pe.wait_ge(fc_split, e * MC + m + 1)
                            need(pe, gated, q * MC + m - 1)
                            for bank, half in ((a_ps[m % 2], 0), (g_ps[m % 2], 1)):
                                first = True
                                for c in range(DC):
                                    for a, b in PASSES:
                                        last = nc.tensor.matmul(bank[:, :],
                                                                fc[a][:, c * 2 + half, m * P:(m + 1) * P],
                                                                xt[b][:, i % 2, c, :], start=first,
                                                                stop=(c == DC - 1 and (a, b) == PASSES[-1]))
                                        first = False
                            last.then_inc(up_done, 1)
                        if i == 0:
                            pe.wait_ge(pj_split, e * MC + MC)
                        for t in range(CT):
                            need(pe, y_ready, q * CT + t - 1)
                            first = True
                            for m in range(MC):
                                if t == 0:
                                    pe.wait_ge(ht_split, q * MC + m + 1)
                                for a, b in PASSES:
                                    last = nc.tensor.matmul(y_ps[t % 2][:, :], ht[a][:, m, t * P:(t + 1) * P],
                                                            pj[b][:, m, :], start=first,
                                                            stop=(m == MC - 1 and (a, b) == PASSES[-1]))
                                    first = False
                            last.then_inc(down_done, 1)
                experts(pe, expert)


def build(nc, x, ctx_t, mask, w_attn, b_qk, b_v, b_o, w_gate, c_fc, c_proj, out):
    xn2_rows = nc.dram_tensor("xn2_rows", [TOKENS + P, D], F32, kind="Internal").ap()
    table = nc.dram_tensor("table", [EXPERTS * CAPACITY, 2], I32, kind="Internal").ap()
    attention_block(nc, x, ctx_t, mask, w_attn, b_qk, b_v, b_o, w_gate, out, xn2_rows, table)
    expert_block(nc, c_fc, c_proj, out, xn2_rows, table)


def kernel(**inputs):
    import numpy as np
    import concourse.bacc as bacc
    from concourse.bass_utils import run_bass_kernel_spmd

    def rows_to_partitions(a, chunks):
        a = a.reshape(a.shape[:-2] + (chunks, P, a.shape[-1]))
        return np.ascontiguousarray(np.swapaxes(a, -3, -2))

    got = {k: np.asarray(a) for k, a in inputs.items()}
    w = "L0_xattn_w"
    arrays = {
        "x": np.ascontiguousarray(got["x"].reshape(TOKENS, D)),
        "ctx_t": rows_to_partitions(np.swapaxes(got["ctx_1024"], 1, 2), DC),
        "mask": np.ascontiguousarray(got["mask_SxS2_bk0"]),
        "w_attn": rows_to_partitions(np.stack([got[w + n].T for n in "qkvo"]), DC),
        "b_qk": np.ascontiguousarray(np.stack([got["L0_xattn_bq"], got["L0_xattn_bk"]]).reshape(2, DC, P)
                                     .transpose(2, 0, 1)),
        "b_v": np.ascontiguousarray(np.broadcast_to(got["L0_xattn_bv"], (P, D))),
        "b_o": np.ascontiguousarray(np.broadcast_to(got["L0_xattn_bo"], (P, D))),
        "w_gate": rows_to_partitions(got["L0_ffn_w_gate"], DC),
        "c_fc": rows_to_partitions(got["L0_ffn_c_fc"], DC),
        "c_proj": rows_to_partitions(got["L0_ffn_c_proj"], MC),
    }
    nc = bacc.Bacc("TRN2", target_bir_lowering=False, num_devices=1)
    args = [nc.dram_tensor(f"in_{n}", a.shape, mybir.dt.from_np(a.dtype), kind="ExternalInput").ap()
            for n, a in arrays.items()]
    out = nc.dram_tensor("out", [TOKENS + P, D], F32, kind="ExternalOutput").ap()
    build(nc, *args, out)
    r = run_bass_kernel_spmd(nc, [{f"in_{n}": a for n, a in arrays.items()}], core_ids=[0])
    return r.results[0]["out"][:TOKENS].reshape(BATCH, SEQ, D)
```
